# Optimizing a Trainium2 kernel written in Bass

```python
import numpy as np
import jax
import jax.numpy as jnp

def _softmax(x, axis=-1):
    return jax.nn.softmax(x, axis=axis)

def _gelu(x):
    return jax.nn.gelu(x, approximate=True)

def _silu(x):
    return jax.nn.silu(x)

def _sigmoid(x):
    return jax.nn.sigmoid(x)

def _layernorm(x, axis=-1, eps=1e-05):
    m = jnp.mean(x, axis=axis, keepdims=True)
    v = jnp.var(x, axis=axis, keepdims=True)
    return (x - m) / jnp.sqrt(v + eps)

def _scatter_add(tgt, idx, src, axis=0):
    return tgt.at[idx].add(src)

def _segment_sum(src, seg, n):
    return jax.ops.segment_sum(src, seg, n)
kernel_name = 'mk_cond_resid_d4_seqx_r8_0bcb24'

def setup_inputs(seed: int=0):
    np.random.seed(seed)
    _w = jnp.asarray

    def _rec_inputs():
        import jax
        import jax.numpy as jnp
        _rk = jax.random.key(seed)
        x = -0.0003929 + 0.9999 * jax.random.normal(jax.random.fold_in(_rk, 1), (64, 32, 512), jnp.float32)
        _lenS = 32 - jax.random.randint(jax.random.fold_in(_rk, 7), (64,), 0, max(1, 32 // 4) + 1, jnp.int32)
        _lenS2 = 32 - jax.random.randint(jax.random.fold_in(_rk, 8), (64,), 0, max(1, 32 // 4) + 1, jnp.int32)
        itok_B_78_3631 = jax.random.randint(jax.random.fold_in(_rk, 11), (64,), 78, 454, jnp.int32)
        itok_B_9_3973 = jax.random.randint(jax.random.fold_in(_rk, 12), (64,), 9, 3974, jnp.int32)
        condB_codebook = -0.0625 + 0.715345 * jax.random.normal(jax.random.fold_in(_rk, 13), (64,), jnp.float32)
        itok_B_0_15 = jax.random.randint(jax.random.fold_in(_rk, 14), (64,), 0, 16, jnp.int32)
        return (x, itok_B_78_3631, itok_B_9_3973, condB_codebook, itok_B_0_15)
    x, itok_B_78_3631, itok_B_9_3973, condB_codebook, itok_B_0_15 = _rec_inputs()

    def _L0_cond_setup():
        import math
        import jax, jax.numpy as jnp
        import numpy as np
        B, H, N, L = (16, 32, 64, 512)
        DT_MIN, DT_MAX = (0.001, 0.1)

        def _get_kernel(log_dt, C, log_A_real, A_imag, length):
            dt = jnp.exp(log_dt)
            Cc = C[..., 0] + 1j * C[..., 1]
            A = -jnp.exp(log_A_real) + 1j * A_imag
            dtA = A * dt[:, None]
            Ct = Cc * (jnp.exp(dtA) - 1.0) / A
            P = dtA[:, :, None] * jnp.arange(length, dtype=jnp.float32)
            K = 2.0 * jnp.einsum('hn,hnl->hl', Ct, jnp.exp(P)).real
            return K
        key = jax.random.key(seed)
        ks = jax.random.split(key, 5)
        u = jax.random.normal(ks[0], (B, H, L), dtype=jnp.float32)
        log_dt = jax.random.uniform(ks[1], (H,), dtype=jnp.float32) * (math.log(DT_MAX) - math.log(DT_MIN)) + math.log(DT_MIN)
        C = jax.random.normal(ks[2], (H, N, 2), dtype=jnp.float32)
        log_A_real = jnp.log(0.5 * jnp.ones((H, N), dtype=jnp.float32))
        A_imag = math.pi * jnp.broadcast_to(jnp.arange(N, dtype=jnp.float32), (H, N))
        D = jax.random.normal(ks[3], (H,), dtype=jnp.float32)
        length = jax.random.randint(ks[4], (B,), 1, L + 1, dtype=jnp.int32)
        return {'u': u, 'log_dt': log_dt, 'C': C, 'log_A_real': log_A_real, 'A_imag': A_imag, 'D': D, 'length': length}
    _L0_cond_all = _L0_cond_setup()
    _L0_cond_in = {k: v for k, v in _L0_cond_all.items() if k in ('log_dt', 'C', 'log_A_real', 'A_imag', 'D')}
    del _L0_cond_all

    def _L1_cond_setup():
        import jax, jax.numpy as jnp
        import numpy as np
        from jax import lax
        B, E, T = (32, 64, 512)
        K = 5
        PAD = (K - 1) // 2
        key = jax.random.key(seed)
        k1, k2, k3 = jax.random.split(key, 3)
        x = jax.random.normal(k1, (B, E, T), dtype=jnp.float32)
        length = jax.random.randint(k2, (B,), 1, T + 1, dtype=jnp.int64)
        conv_w = jax.random.normal(k3, (1, 1, K), dtype=jnp.float32) * (1.0 / np.sqrt(K))
        return {'x': x, 'length': length, 'conv_w': conv_w}
    _L1_cond_all = _L1_cond_setup()
    _L1_cond_in = {k: v for k, v in _L1_cond_all.items() if k in ('conv_w',)}
    del _L1_cond_all

    def _L2_cond_setup():
        import jax, jax.numpy as jnp
        import numpy as np
        GROUP = 128
        LORA_ALPHA = 32.0
        LORA_RANK = 64
        key = jax.random.key(seed)
        k1, k2, k3, k4 = jax.random.split(key, 4)
        O, I = (512, 512)
        x = jax.random.normal(k1, (4, 256, I), dtype=jnp.float32)
        weight = jax.random.normal(k2, (O, I), dtype=jnp.float32) * 0.02
        wg = weight.reshape(O, I // GROUP, GROUP)
        scale_log = jnp.log(jnp.clip(jnp.max(jnp.abs(wg), axis=2, keepdims=True), 1e-05))
        codebook = jnp.array([-1.0, -0.25, 0.0, 1.0], dtype=jnp.float32)
        lora_A = jax.random.normal(k3, (LORA_RANK, I), dtype=jnp.float32) * 0.02
        lora_B = jax.random.normal(k4, (O, LORA_RANK), dtype=jnp.float32) * 0.02
        return {'x': x, 'weight': weight, 'scale_log': scale_log, 'codebook': codebook, 'lora_A': lora_A, 'lora_B': lora_B}
    _L2_cond_all = _L2_cond_setup()
    _L2_cond_in = {k: v for k, v in _L2_cond_all.items() if k in ('weight', 'scale_log', 'lora_A', 'lora_B')}
    del _L2_cond_all

    def _L3_cond_setup():
        import jax, jax.numpy as jnp
        import numpy as np
        NUM_CONDITIONS = 16
        IN_CH = 32
        OUT_CH = 32
        B = 64
        T = 512
        key = jax.random.key(seed)
        k_x, k_w, k_c = jax.random.split(key, 3)
        x = jax.random.normal(k_x, (B, IN_CH, T), dtype=jnp.float32)
        bound = float(np.sqrt(6.0 / IN_CH))
        weights = jax.random.uniform(k_w, (NUM_CONDITIONS, IN_CH, OUT_CH), dtype=jnp.float32, minval=-bound, maxval=bound)
        condition = jax.random.randint(k_c, (B,), 0, NUM_CONDITIONS, dtype=jnp.int64)
        return {'x': x, 'weights': weights, 'condition': condition}
    _L3_cond_all = _L3_cond_setup()
    _L3_cond_in = {k: v for k, v in _L3_cond_all.items() if k in ('weights',)}
    del _L3_cond_all
    return {'x': x, 'itok_B_78_3631': itok_B_78_3631, 'itok_B_9_3973': itok_B_9_3973, 'condB_codebook': condB_codebook, 'itok_B_0_15': itok_B_0_15, 'L0_cond_log_dt': _L0_cond_in['log_dt'], 'L0_cond_C': _L0_cond_in['C'], 'L0_cond_log_A_real': _L0_cond_in['log_A_real'], 'L0_cond_A_imag': _L0_cond_in['A_imag'], 'L0_cond_D': _L0_cond_in['D'], 'L1_cond_conv_w': _L1_cond_in['conv_w'], 'L2_cond_weight': _L2_cond_in['weight'], 'L2_cond_scale_log': _L2_cond_in['scale_log'], 'L2_cond_lora_A': _L2_cond_in['lora_A'], 'L2_cond_lora_B': _L2_cond_in['lora_B'], 'L3_cond_weights': _L3_cond_in['weights']}

def reference(x, itok_B_78_3631, itok_B_9_3973, condB_codebook, itok_B_0_15, L0_cond_log_dt, L0_cond_C, L0_cond_log_A_real, L0_cond_A_imag, L0_cond_D, L1_cond_conv_w, L2_cond_weight, L2_cond_scale_log, L2_cond_lora_A, L2_cond_lora_B, L3_cond_weights):
    import jax
    import jax.numpy as jnp

    def _L0_cond_ref(u, log_dt, C, log_A_real, A_imag, D, length):
        import math
        import jax, jax.numpy as jnp
        import numpy as np
        B, H, N, L = (16, 32, 64, 512)
        DT_MIN, DT_MAX = (0.001, 0.1)

        def _get_kernel(log_dt, C, log_A_real, A_imag, length):
            dt = jnp.exp(log_dt)
            Cc = C[..., 0] + 1j * C[..., 1]
            A = -jnp.exp(log_A_real) + 1j * A_imag
            dtA = A * dt[:, None]
            Ct = Cc * (jnp.exp(dtA) - 1.0) / A
            P = dtA[:, :, None] * jnp.arange(length, dtype=jnp.float32)
            K = 2.0 * jnp.einsum('hn,hnl->hl', Ct, jnp.exp(P)).real
            return K
        Bq, Hq, Lq = u.shape
        K = _get_kernel(log_dt, C, log_A_real, A_imag, Lq)
        n = 2 * Lq
        kf = jnp.fft.rfft(K, n=n)
        uf = jnp.fft.rfft(u, n=n)
        y = jnp.fft.irfft(uf * kf[None], n=n)[..., :Lq]
        y = y + u * D[:, None]
        mask = (jnp.arange(Lq)[None, :] < length[:, None]).astype(u.dtype)
        return y * mask[:, None, :]

    def _L1_cond_ref(x, length, conv_w):
        import jax, jax.numpy as jnp
        import numpy as np
        from jax import lax
        B, E, T = (32, 64, 512)
        K = 5
        PAD = (K - 1) // 2
        mask = (jnp.arange(T)[None, :] < length[:, None]).astype(x.dtype)
        denom = length.astype(x.dtype)[:, None]
        y = jnp.einsum('bet,bt->be', x, mask) / denom
        yc = lax.conv_general_dilated(y[:, None, :], conv_w, window_strides=(1,), padding=[(PAD, PAD)], dimension_numbers=('NCH', 'OIH', 'NCH'))[:, 0, :]
        gate = jax.nn.sigmoid(yc)
        return x * gate[:, :, None]

    def _L2_cond_ref(x, weight, scale_log, codebook, lora_A, lora_B):
        import jax, jax.numpy as jnp
        import numpy as np
        GROUP = 128
        LORA_ALPHA = 32.0
        LORA_RANK = 64
        O, I = weight.shape
        lora_delta = lora_B @ lora_A * (LORA_ALPHA / LORA_RANK)
        cb = codebook / jnp.clip(jnp.max(jnp.abs(codebook)), 1e-08)
        scale = jnp.exp(scale_log)
        wg = (weight + lora_delta).reshape(O, I // GROUP, GROUP)
        normalized = wg / scale
        thresholds = (cb[:-1] + cb[1:]) * 0.5
        idx = jnp.searchsorted(thresholds, normalized, side='left')
        quantized = cb[idx]
        w = jax.lax.stop_gradient(quantized - normalized) + normalized
        w_q = (w * scale).reshape(O, I)
        w_eff = w_q + lora_delta
        return x @ w_eff.T

    def _L3_cond_ref(x, weights, condition):
        import jax, jax.numpy as jnp
        import numpy as np
        NUM_CONDITIONS = 16
        IN_CH = 32
        OUT_CH = 32
        B = 64
        T = 512
        W = weights[condition]
        return jnp.einsum('bct,bcd->bdt', x, W)
    x = x + _L0_cond_ref(x, L0_cond_log_dt, L0_cond_C, L0_cond_log_A_real, L0_cond_A_imag, L0_cond_D, itok_B_78_3631)
    x = x + _L1_cond_ref(x, itok_B_9_3973, L1_cond_conv_w)
    x = x + _L2_cond_ref(x, L2_cond_weight, L2_cond_scale_log, condB_codebook, L2_cond_lora_A, L2_cond_lora_B)
    x = x + _L3_cond_ref(x, L3_cond_weights, itok_B_0_15)
    return x

_drawn_inputs = setup_inputs


def setup_inputs(seed=0):
    import zlib

    import numpy as np

    out = dict(_drawn_inputs(seed))
    spreads = {'L0_cond_log_A_real': (-0.6931471824645996, 0.2)}
    factors = {}
    for name, (base, spread) in spreads.items():
        noise = np.random.default_rng([zlib.crc32(name.encode()), seed]).standard_normal(out[name].shape)
        drawn = base * np.exp(spread * noise) if base else spread * noise
        out[name] = jnp.asarray(drawn.astype(out[name].dtype))
    for name, factor in factors.items():
        out[name] = (out[name] * factor).astype(out[name].dtype)
    return out
```

```python
from contextlib import ExitStack

import concourse.bass as bass
from concourse import mybir

ALU = mybir.AluOpType
ACT = mybir.ActivationFunctionType
F32 = mybir.dt.float32
I32 = mybir.dt.int32
AX_X = mybir.AxisListType.X

P = 128
TWO_PI = 6.2831850
ROUND = 12582912.0
BIG = 3.0e38
LN2_HI, LN2_LO = 0.693359375, -2.12194440e-4
PI2_A, PI2_B, PI2_C = 6.28125, 1.9350051879882812e-3, 3.0199159819e-7
MIX_LAG = 5
FAST_SLOTS = 4


def cond_resid_kernel(nc, x, len_conv, len_gate, codebook, cond, log_dt, C, log_A_real, A_imag, D, conv_w,
                      weight, scale_log, lora_A, lora_B, cond_W, out):
    B, H, L = x.shape
    N = A_imag.shape[1]
    NC = L // P
    GB = P // H
    NG = B // GB
    NPAIR = H // 2
    NCODE = codebook.shape[0]
    NTH = NCODE - 1
    R = lora_A.shape[0]
    NK = cond_W.shape[0]
    TAPS = conv_w.shape[2]
    AS, RS = L // 32, 32
    NSLOT = 3
    PAD = L + P

    with ExitStack() as ctx:
        def sb(name, shape, dt=F32):
            return ctx.enter_context(nc.sbuf_tensor(name, shape, dt))

        def sem(name):
            return ctx.enter_context(nc.semaphore(name))

        psX = [ctx.enter_context(nc.psum_tensor(f"psX{i}", [P, 512], F32)) for i in range(2)]
        psA = ctx.enter_context(nc.psum_tensor("psA", [P, 512], F32))
        psB = ctx.enter_context(nc.psum_tensor("psB", [P, 512], F32))
        psC = [ctx.enter_context(nc.psum_tensor(f"psC{i}", [P, 512], F32)) for i in range(4)]

        kpad = nc.dram_tensor("kpad", [H, PAD], F32, kind="Internal")
        wsel_dram = nc.dram_tensor("wsel_dram", [B, H * H], F32, kind="Internal")

        xrows = sb("xrows", [P, NG, L])
        w_in = sb("w_in", [P, 4, L])
        la = sb("la", [R, L])
        lb = sb("lb", [P, 4, R])
        lns = sb("lns", [P, 1 + N + 16])
        bim = sb("bim", [P, N])
        cin = sb("cin", [P, N, 2])
        drow = sb("drow", [1, H, RS])
        dcol = sb("dcol", [1, H])
        last_a = sb("last_a", [P, AS])
        cb = sb("cb", [P, NCODE])
        cwt = sb("cwt", [P, TAPS])
        leni = sb("leni", [P, 2, B], I32)
        condi = sb("condi", [NK, B], I32)
        wall = sb("wall", [NK, H * H])

        diff = sb("diff", [P, P])
        ident = sb("ident", [P, P])
        tri = sb("tri", [P, P])
        own = sb("own", [P, GB])
        pcol = sb("pcol", [P, 1])
        ramp = sb("ramp", [P, 64])
        ramp1 = sb("ramp1", [P, 64])
        phase = sb("phase", [P, 1])
        phase_rad = sb("phase_rad", [P, 1])
        quarter_rad = sb("quarter_rad", [P, 1])
        ones = sb("ones", [P, P])
        zpad = sb("zpad", [H, P])

        ex = sb("ex", [P, 6, 1 + N + 16])
        exi = sb("exi", [P, 1 + N + 16], I32)
        pm = sb("pm", [H, 24, N])
        pp = sb("pp", [H, 4, 2 * N])
        par = sb("par", [P, 4, H])
        sq = sb("sq", [P, 8, H])
        magV = sb("magV", [P, H, RS])
        magU = sb("magU", [P, H, AS])
        tau32 = sb("tau32", [P, 2, H])
        tV = sb("tV", [P, H, RS])
        tU = sb("tU", [P, H, AS])
        fV = sb("fV", [P, H, RS])
        fU = sb("fU", [P, 2, H, AS])
        sV, sU = fV, fU
        ksb = sb("ksb", [AS, H, RS])

        th = sb("th", [P, 64])
        tp = sb("tp", [P, 65])
        act_row = sb("act_row", [P, 64])
        scr = sb("scr", [P, 4, 64])
        small = sb("small", [P, 16])
        slot_rhs = sb("slot_rhs", [64, 2, 64])
        slots = sb("slots", [P, 2, 64])
        over = sb("over", [P, 64])
        n_int = sb("n_int", [P, 1], I32)
        cur = sb("cur", [P, 3])
        inv_scale = sb("inv_scale", [P, 16])
        lbT = sb("lbT", [R, L])
        dlt = sb("dlt", [P, 4, L])
        nrm = sb("nrm", [P, 4, L])
        msk = sb("msk", [P, 4, L], I32)
        quant = sb("quant", [P, 4, L])
        mt = msk[:, :, :].bitcast(F32)

        lenf = sb("lenf", [P, 2, B])
        keep = sb("keep", [P, NC, B], I32)
        mask2 = sb("mask2", [P, NC, B])
        linv = sb("linv", [P, B])
        xT = sb("xT", [P, NC, NG, H, GB])
        toep = sb("toep", [P, NSLOT, 2, L])
        hank = sb("hank", [P, NSLOT, 2, L])
        cmat = sb("cmat", [P, P])
        ctmp = sb("ctmp", [P, P])
        lown = sb("lown", [P, NG, GB])
        linv_own = sb("linv_own", [P, NG])
        mtmp = fU[:, 0, :, :].rearrange("p h a -> p (h a)")
        mhalf = tV[:, :, :].rearrange("p h r -> p (h r)").rearrange("p (s n) -> p s n", s=4)
        msum = w_in[:, :, :].rearrange("p t i -> p (t i)").rearrange("p (g n) -> p g n", g=NG)
        gmean = sb("gmean", [P, NG])
        gth = sb("gth", [P, NG])
        gate = sb("gate", [P, NG])
        condf = sb("condf", [NK, B])
        onehot = sb("onehot", [NK, B])
        wsel = sb("wsel", [B, H * H])
        wrows = sb("wrows", [P, NG, H])
        gmat = xrows[:, 12:16, :].rearrange("p s l -> p (s l)").rearrange("p (g n) -> p g n", g=NG)
        ysb = xrows[:, 0:8, :]
        osb = xrows[:, 8:12, :]

        S = {n: sem(n) for n in (
            "in_lns in_imag in_c in_d in_cb in_cw in_len in_cond in_w in_la in_lb in_wall "
            "consts pool_chain par_chain thr_chain dve_chain dve_loop "
            "drow_ready pad_written k_written tanh_in tanh_done trig_in trig_done params params_T par_ready mags "
            "sinV_in sinU_in sin_done kfac k_done ksb_ready scale_ready raw_ready norm_ready "
            "lbT_done lbT_sb delta_done delta_sb sel_oh sel_done sel_sb sel_written sel_loaded "
            "xt_done xt_sb slot_ready slot_done turned conv_done conv_used mhalf_ready mhalf_used msum_ready "
            "weff wT_done wT_sb masks cmat_ready ymean gmean_ready chan gate_th gated "
            "y_done y_sb o_done o_sb").split()}
        k_written = [sem(f"k_written{i}") for i in range(2)]
        in_x = [sem(f"in_x{i}") for i in range(NG)]
        in_hank = [sem(f"in_hank{i}") for i in range(NSLOT)]
        stored = [sem(f"stored{i}") for i in range(4)]

        x_rows = x.rearrange("(g b) h l -> g h b l", b=GB)
        o_rows = out.rearrange("(g b) h l -> g h b l", b=GB)

        def hankel_rows(i):
            return bass.AP(kpad, 2 * i * PAD, [[1, P], [PAD, 2], [1, L]])

        block = ctx.enter_context(nc.Block())

        @block.sync
        def _(sp):
            sp.dma_start(lns[:, 1:1 + N], bass.AP(log_A_real.tensor, 0, [[0, GB], [N, H], [1, N]])).then_inc(S["in_lns"], 16)
            sp.dma_start(lns[:, 0:1], bass.AP(log_dt.tensor, 0, [[0, GB], [1, H], [1, 1]])).then_inc(S["in_lns"], 16)
            sp.dma_start(lns[:, 1 + N:].rearrange("p (t g) -> p t g", t=4),
                         scale_log.rearrange("(t p) g k -> p t (g k)", p=P)).then_inc(S["in_lns"], 16)
            sp.dma_start(bim[:, :], bass.AP(A_imag.tensor, 0, [[0, GB], [N, H], [1, N]])).then_inc(S["in_imag"], 16)
            sp.dma_start(cin[:, :, :], bass.AP(C.tensor, 0, [[0, GB], [2 * N, H], [2, N], [1, 2]])).then_inc(S["in_c"], 16)
            for g in range(NG):
                sp.dma_start(xrows[:, g, :], x_rows[g]).then_inc(in_x[g], 16)
            sp.wait_ge(S["consts"], 1)
            sp.dma_start(kpad[:, L:PAD], zpad[:, :]).then_inc(S["pad_written"], 16)
            sp.wait_ge(S["sel_sb"], 2)
            sp.dma_start(wsel_dram[:, :], wsel[:, :]).then_inc(S["sel_written"], 16)
            sp.wait_ge(S["sel_written"], 16)
            for b in range(GB):
                sp.dma_start(wrows[b:P:GB, :, :], bass.AP(wsel_dram, b * H * H, [[H, H], [GB * H * H, NG], [1, H]])
                             ).then_inc(S["sel_loaded"], 16)
            sp.wait_ge(S["pad_written"], 16)
            for i in range(NPAIR):
                if i % (NPAIR // 2) == 0:
                    sp.wait_ge(k_written[i // (NPAIR // 2)], 16)
                if i >= NSLOT:
                    sp.wait_ge(S["turned"], i - NSLOT + 1)
                sp.dma_start(hank[:, i % NSLOT, :, :], hankel_rows(i)).then_inc(in_hank[i % NSLOT], 16)
            for g in range(NG):
                sp.wait_ge(S["o_sb"], g + 1)
                sp.dma_start(o_rows[g], osb[:, g % 4, :]).then_inc(stored[g % 4], 16)
            for i in range(4):
                sp.wait_ge(stored[i], 16 * (NG // 4))

        @block.gpsimd
        def _(pool):
            n = [0]

            def link(ins):
                n[0] += 1
                ins.then_inc(S["pool_chain"], 1)
                pool.wait_ge(S["pool_chain"], n[0])

            g = nc.gpsimd
            g.iota(diff[:, :], [[1, P]], base=0, channel_multiplier=-1, allow_small_or_imprecise_dtypes=True)
            g.iota(pcol[:, :], [[0, 1]], base=0, channel_multiplier=1, allow_small_or_imprecise_dtypes=True)
            g.iota(ramp[:, :], [[1, 64]], base=0, channel_multiplier=0, allow_small_or_imprecise_dtypes=True)
            link(g.iota(ramp1[:, :], [[1, 64]], base=1, channel_multiplier=0, allow_small_or_imprecise_dtypes=True))
            g.tensor_scalar(tri[:, :], diff[:, :], 0.0, None, ALU.is_le)
            g.tensor_scalar(ident[:, :], diff[:, :], 0.0, None, ALU.is_equal)
            g.memset(zpad[:, :], 0.0)
            g.memset(ones[:, :], 1.0)
            g.memset(quarter_rad[:, :], 0.25 * TWO_PI)
            g.tensor_scalar(phase[:, :], pcol[:, :], float(N), 0.25, ALU.is_lt, ALU.mult)
            g.tensor_scalar(phase_rad[:, :], pcol[:, :], float(N), 0.25 * TWO_PI, ALU.is_lt, ALU.mult)
            g.tensor_scalar(last_a[:, :], ramp[:, 0:AS], float(AS - 1), None, ALU.is_equal).then_inc(S["consts"], 1)
            link(g.memset(drow[:, :, :], 0.0))
            pool.wait_ge(S["in_d"], 16)
            g.tensor_scalar(drow[:, :, 0], dcol[:, :], 1.0, None, ALU.add).then_inc(S["drow_ready"], 1)
            pool.wait_ge(S["in_cond"], 16)
            link(g.tensor_copy(condf[:, :], condi[:, :]))
            g.tensor_scalar(onehot[:, :], condf[:, :], pcol[0:NK, 0:1], None, ALU.is_equal).then_inc(S["sel_oh"], 1)
            pool.wait_ge(S["in_len"], 32)
            link(g.tensor_copy(lenf[:, :, :], leni[:, :, :]))
            for c in range(NC):
                g.tensor_scalar(keep[:, c, :], lenf[:, 0, :], pcol[:, 0:1], float(P * c), ALU.subtract, ALU.is_gt)
                last = g.tensor_scalar(mask2[:, c, :], lenf[:, 1, :], pcol[:, 0:1], float(P * c), ALU.subtract, ALU.is_gt)
            last.then_inc(S["masks"], 1)

            link(g.memset(magV[:, :, 0:1], 1.0))
            link(g.memset(magU[:, :, 0:1], 1.0))
            pool.wait_ge(S["par_ready"], 1)
            pows = [par[:, 2, :]]
            for k in range(8):
                link(g.tensor_tensor(sq[:, k, :], pows[k], pows[k], ALU.mult))
                pows.append(sq[:, k, :])
            for k in range(4):
                w = 1 << k
                link(g.tensor_tensor(magU[:, :, w:2 * w], magU[:, :, 0:w],
                                     pows[5 + k].unsqueeze(2).to_broadcast([P, H, w]), ALU.mult))
            for k in range(5):
                w = 1 << k
                last = g.tensor_tensor(magV[:, :, w:2 * w], magV[:, :, 0:w],
                                       pows[k].unsqueeze(2).to_broadcast([P, H, w]), ALU.mult)
                if k < 4:
                    link(last)
            last.then_inc(S["mags"], 1)
            pool.wait_ge(S["in_w"], 16)
            pool.wait_ge(S["delta_sb"], 4)
            for t in range(4):
                g.tensor_tensor(w_in[:, t, :], w_in[:, t, :], dlt[:, t, :], ALU.add).then_inc(S["raw_ready"], 1)
            pool.wait_ge(S["in_cw"], 16)
            for k in range(TAPS):
                link(g.tensor_scalar(ctmp[:, :], diff[:, :], float(GB * (TAPS // 2 - k)), cwt[:, k:k + 1], ALU.is_equal, ALU.mult))
                if k == 0:
                    link(g.tensor_copy(cmat[:, :], ctmp[:, :]))
                elif k < TAPS - 1:
                    link(g.tensor_tensor(cmat[:, :], cmat[:, :], ctmp[:, :], ALU.add))
                else:
                    g.tensor_tensor(cmat[:, :], cmat[:, :], ctmp[:, :], ALU.add).then_inc(S["cmat_ready"], 1)
            half = NC // 2 * NG * 2 * GB
            for i in range(NPAIR):
                pool.wait_ge(S["conv_used"], i + 1)
                if i > 0:
                    pool.wait_ge(S["mhalf_ready"], i)
                link(g.tensor_tensor(
                    mtmp.rearrange("p (n h b) -> p n h b", h=2, b=GB),
                    xT[:, :, :, 2 * i:2 * i + 2, :].rearrange("p c g h b -> p (c g) h b"),
                    mask2[:, :, :].rearrange("p c (g b) -> p (c g) b", b=GB).unsqueeze(2).to_broadcast([P, NC * NG, 2, GB]),
                    ALU.mult))
                if i >= 4:
                    pool.wait_ge(S["mhalf_used"], i - 3)
                g.tensor_tensor(mhalf[:, i % 4, :], mtmp[:, 0:half], mtmp[:, half:], ALU.add).then_inc(S["mhalf_ready"], 1)

        @block.scalar
        def _(act):
            a = nc.scalar
            act.dma_start(cb[:, :], bass.AP(codebook.tensor, 0, [[0, P], [1, NCODE]])).then_inc(S["in_cb"], 16)
            act.dma_start(condi[:, :], bass.AP(cond.tensor, 0, [[0, NK], [1, B]])).then_inc(S["in_cond"], 16)
            act.dma_start(dcol[:, :], D.rearrange("(o h) -> o h", o=1)).then_inc(S["in_d"], 16)
            act.dma_start(lb[:, :, :], lora_B.rearrange("(t p) r -> p t r", p=P)).then_inc(S["in_lb"], 16)
            act.dma_start(la[:, :], lora_A).then_inc(S["in_la"], 16)
            act.dma_start(leni[:, 0, :], bass.AP(len_conv.tensor, 0, [[0, P], [1, B]])).then_inc(S["in_len"], 16)
            act.dma_start(leni[:, 1, :], bass.AP(len_gate.tensor, 0, [[0, P], [1, B]])).then_inc(S["in_len"], 16)
            act.dma_start(wall[:, :], cond_W.rearrange("k c d -> k (c d)")).then_inc(S["in_wall"], 16)
            act.dma_start(cwt[:, :], bass.AP(conv_w.tensor, 0, [[0, P], [1, TAPS]])).then_inc(S["in_cw"], 16)
            act.dma_start(w_in[:, :, :], weight.rearrange("(t p) i -> p t i", p=P)).then_inc(S["in_w"], 16)

            def x_evac(g):
                act.wait_ge(S["xt_done"], g + 1)
                dst = xT[:, :, g, :, :].rearrange("p c h b -> p c (h b)")
                a.copy(dst, psX[g % 2][:, :].rearrange("p (c n) -> p c n", c=NC)).then_inc(S["xt_sb"], 1)

            act.wait_ge(S["lbT_done"], 1)
            a.mul(lbT[:, :], psB[0:R, :], 0.5).then_inc(S["lbT_sb"], 1)
            act.wait_ge(S["tanh_in"], 1)
            a.activation(pm[:, 7, :], pm[:, 0, :], ACT.Tanh, scale=0.5).then_inc(S["tanh_done"], 1)
            act.wait_ge(S["trig_in"], 1)
            a.activation(pm[:, 6, :], pm[:, 4, :], ACT.Sin, scale=0.5).then_inc(S["trig_done"], 1)
            a.activation(pm[:, 5, :], pm[:, 4, :], ACT.Sin).then_inc(S["trig_done"], 1)
            for t in range(4):
                act.wait_ge(S["delta_done"], t + 1)
                a.copy(dlt[:, t, :], psC[t][:, :]).then_inc(S["delta_sb"], 1)
            for i in range(2):
                act.wait_ge(S["sel_done"], i + 1)
                a.copy(wsel[:, i * 512:(i + 1) * 512], psX[i][0:B, :]).then_inc(S["sel_sb"], 1)
            act.wait_ge(S["consts"], 1)
            for g in range(NG):
                x_evac(g)
                if g == 2:
                    act.wait_ge(S["sinU_in"], 1)
                    a.activation(sU[:, 0, :, :], fU[:, 0, :, :], ACT.Sin, bias=quarter_rad[:, 0:1],
                                 scale=-TWO_PI).then_inc(S["sin_done"], 1)
                if g == 3:
                    act.wait_ge(S["sinU_in"], 2)
                    a.activation(sU[:, 1, :, :], fU[:, 1, :, :], ACT.Sin, scale=-TWO_PI).then_inc(S["sin_done"], 1)
                if g == 6:
                    act.wait_ge(S["sinV_in"], 1)
                    a.activation(sV[:, :, :], fV[:, :, :], ACT.Sin, bias=phase_rad[:, 0:1],
                                 scale=-TWO_PI).then_inc(S["sin_done"], 1)
            act.wait_ge(S["scale_ready"], 1)

            def normalize(t):
                act.wait_ge(S["raw_ready"], t + 1)
                for q in range(4):
                    last = a.activation(nrm[:, t, q * P:(q + 1) * P], w_in[:, t, q * P:(q + 1) * P], ACT.Copy,
                                        scale=inv_scale[:, 4 * t + q:4 * t + q + 1])
                last.then_inc(S["norm_ready"], 1)

            def kernels_out(k, bank):
                act.wait_ge(S["k_done"], k + 1)
                hs = slice(k * H // 2, (k + 1) * H // 2)
                a.copy(ksb[:, hs, ::-1], bank[0:AS, :].rearrange("a (h r) -> a h r", r=RS)).then_inc(S["ksb_ready"], 1)
                act.wait_ge(S["ksb_ready"], k + 1)
                act.dma_start(bass.AP(kpad, k * (H // 2) * PAD, [[RS, AS], [PAD, H // 2], [1, RS]]),
                              ksb[:, hs, :]).then_inc(k_written[k], 16)

            normalize(0)
            normalize(1)
            kernels_out(0, psA)
            normalize(2)
            kernels_out(1, psB)
            normalize(3)
            for i in range(NPAIR):
                act.wait_ge(in_hank[i % NSLOT], 16 * (i // NSLOT + 1))
                if i >= NSLOT:
                    act.wait_ge(S["conv_done"], i - NSLOT + 1)
                a.copy(toep[:, i % NSLOT, :, :], hank[:, i % NSLOT, :, ::-1]).then_inc(S["turned"], 1)
            for c in range(NC):
                act.wait_ge(S["wT_done"], c + 1)
                a.copy(mt[:, c, :], psX[c % 2][:, :]).then_inc(S["wT_sb"], 1)
            for g in range(NG):
                act.wait_ge(S["y_done"], g + 1)
                if g >= 8:
                    act.wait_ge(S["o_done"], g - 7)
                a.copy(ysb[:, g % 8, :], psC[g % 4][:, :]).then_inc(S["y_sb"], 1)
                if g == 2:
                    act.wait_ge(S["chan"], 1)
                    a.activation(gth[:, :], psB[:, 0:NG], ACT.Tanh, scale=0.5).then_inc(S["gate_th"], 1)

        @block.vector
        def _(dve):
            v = nc.vector
            n = {"par_chain": 0, "thr_chain": 0}

            def chained(name):
                def step(op, *args):
                    if n[name]:
                        dve.wait_ge(S[name], n[name])
                    op(*args).then_inc(S[name], 1)
                    n[name] += 1
                return step

            par_step, thr_step = chained("par_chain"), chained("thr_chain")

            mx, mn, cnt, rank, actc, tcol, ccol = (small[:, i:i + 1] for i in range(7))
            v.memset(tp[:, 0:1], -BIG)
            v.memset(tp[:, 64:65], BIG)
            dve.wait_ge(S["in_cb"], 16)
            thr_step(v.tensor_reduce, mx, cb[:, :], AX_X, ALU.max)
            thr_step(v.tensor_reduce, mn, cb[:, :], AX_X, ALU.min)
            thr_step(v.scalar_tensor_tensor, mx, mn, -1.0, mx, ALU.mult, ALU.max)
            thr_step(v.tensor_scalar, mx, mx, 1e-8, None, ALU.max)

            y, k, r, p = (ex[:, i, :] for i in range(4))
            dve.wait_ge(S["in_lns"], 48)
            par_step(v.tensor_scalar, y, lns[:, :], -87.0, 88.0, ALU.max, ALU.min)
            thr_step(v.reciprocal, mx, mx)
            par_step(v.tensor_scalar, k, y, 1.4426950408889634, ROUND, ALU.mult, ALU.add)
            thr_step(v.tensor_scalar, cb[:, :], cb[:, :], mx, None, ALU.mult)
            par_step(v.tensor_scalar, k, k, ROUND, None, ALU.subtract)
            thr_step(v.tensor_tensor, th[:, 1:64], cb[:, 0:NTH], cb[:, 1:NCODE], ALU.add)
            par_step(v.scalar_tensor_tensor, r, k, -LN2_HI, y, ALU.mult, ALU.add)
            thr_step(v.tensor_scalar, th[:, 1:64], th[:, 1:64], 0.5, None, ALU.mult)
            par_step(v.scalar_tensor_tensor, r, k, -LN2_LO, r, ALU.mult, ALU.add)

            def tree(level):
                s = 32 >> level
                return tp[:, s:64:2 * s], th[:, s:64:2 * s], tp[:, 0:64:2 * s], tp[:, 2 * s:65:2 * s]

            def clip_low(level):
                mid, own_th, low, _ = tree(level)
                thr_step(v.tensor_tensor, mid, own_th, low, ALU.max)

            def clip_high(level):
                mid, _, _, high = tree(level)
                thr_step(v.tensor_tensor, mid, mid, high, ALU.min)

            clip_low(0)
            par_step(v.tensor_scalar, exi[:, :], k, 127.0, None, ALU.add)
            clip_high(0)
            par_step(v.tensor_scalar, p, r, 1.0 / 5040, None, ALU.mult)
            clip_low(1)
            par_step(v.tensor_scalar, exi[:, :], exi[:, :], 23, None, ALU.logical_shift_left)
            clip_high(1)
            for level, c in ((2, 720), (3, 24), (4, 2)):
                par_step(v.scalar_tensor_tensor, p, p, 1.0 / c, r, ALU.add, ALU.mult)
                clip_low(level)
                par_step(v.scalar_tensor_tensor, p, p, 1.0 / {720: 120, 24: 6, 2: 1}[c], r, ALU.add, ALU.mult)
                clip_high(level)
            e = ex[:, 4, :]
            par_step(v.scalar_tensor_tensor, e, p, 1.0, exi[:, :].bitcast(F32), ALU.add, ALU.mult)
            clip_low(5)
            dt, aa = e[0:H, 0:1], e[0:H, 1:1 + N]
            scale = e[:, 1 + N:]

            xx, w, kk, wr, wc, s1, s2, tt = (pm[:, i, :] for i in (0, 1, 2, 3, 4, 5, 6, 7))
            bb = bim[0:H, :]
            dve.wait_ge(S["par_chain"], n["par_chain"])
            v.tensor_scalar(xx, aa, dt, -1.0, ALU.mult, ALU.mult).then_inc(S["tanh_in"], 1)
            clip_high(5)
            dve.wait_ge(S["in_imag"], 16)
            par_step(v.tensor_scalar, w, bb, dt, None, ALU.mult)
            thr_step(v.tensor_tensor, act_row[:, 0:NTH], tp[:, 1:64], tp[:, 2:65], ALU.is_lt)
            par_step(v.tensor_scalar, kk, w, 0.15915494309189535, ROUND, ALU.mult, ALU.add)
            thr_step(v.tensor_reduce, cnt, act_row[:, 0:NTH], AX_X, ALU.add)
            par_step(v.tensor_scalar, kk, kk, ROUND, None, ALU.subtract)
            dve.wait_ge(S["consts"], 1)
            thr_step(v.tensor_tensor, scr[0:NTH, 0, 0:NTH], act_row[0:NTH, 0:NTH], tri[0:NTH, 0:NTH], ALU.mult)
            par_step(v.scalar_tensor_tensor, wr, kk, -PI2_A, w, ALU.mult, ALU.add)
            thr_step(v.tensor_tensor, scr[0:NTH, 1, 0:NTH], act_row[0:NTH, 0:NTH], ident[0:NTH, 0:NTH], ALU.mult)
            par_step(v.scalar_tensor_tensor, wr, kk, -PI2_B, wr, ALU.mult, ALU.add)
            thr_step(v.tensor_tensor, scr[0:NTH, 2, 0:NTH], tp[0:NTH, 1:64], ident[0:NTH, 0:NTH], ALU.mult)
            par_step(v.scalar_tensor_tensor, wr, kk, -PI2_C, wr, ALU.mult, ALU.add)
            dve.wait_ge(S["par_chain"], n["par_chain"])
            v.tensor_scalar(wc, wr, -3.1415925, 3.1415925, ALU.max, ALU.min).then_inc(S["trig_in"], 1)
            em, q = pm[:, 11, :], pm[:, 13, :]
            dve.wait_ge(S["tanh_done"], 1)
            par_step(v.tensor_scalar, em, tt, -1.0, 1.0, ALU.mult, ALU.add)
            thr_step(v.tensor_tensor, scr[0:NTH, 3, 0:NTH], cb[0:NTH, 1:NCODE], ident[0:NTH, 0:NTH], ALU.mult)
            par_step(v.reciprocal, em, em)
            thr_step(v.tensor_reduce, small[0:NTH, 3:7], scr[0:NTH, :, 0:NTH], AX_X, ALU.add)
            par_step(v.scalar_tensor_tensor, em, tt, 2.0, em, ALU.mult, ALU.mult)
            thr_step(v.tensor_scalar, small[0:NTH, 5:7], small[0:NTH, 5:7], actc[0:NTH, :], None, ALU.mult)
            ep = pp[:, 2, 0:N]
            par_step(v.tensor_scalar, pp[:, 2, 0:N], em, 1.0, None, ALU.add)
            v.tensor_scalar(pp[:, 2, N:], em, 1.0, None, ALU.add)
            v.tensor_scalar(pp[:, 3, 0:N], wr, 0.15915494309189535, None, ALU.mult)
            v.tensor_scalar(pp[:, 3, N:], wr, 0.15915494309189535, None, ALU.mult).then_inc(S["params"], 1)

            dve.wait_ge(S["trig_done"], 1)
            thr_step(v.tensor_scalar, slot_rhs[0:NTH, 0, :], ramp1[0:NTH, :], rank[0:NTH, :], tcol[0:NTH, :], ALU.is_equal, ALU.mult)
            par_step(v.tensor_tensor, q, s2, s2, ALU.mult)
            v.tensor_copy(n_int[:, :], cnt)
            thr_step(v.tensor_scalar, slot_rhs[0:NTH, 1, :], ramp1[0:NTH, :], rank[0:NTH, :], ccol[0:NTH, :], ALU.is_equal, ALU.mult)
            v.tensor_scalar(over[:, :], ramp1[:, :], cnt, BIG, ALU.is_gt, ALU.mult).then_inc(S["slot_ready"], 1)
            par_step(v.scalar_tensor_tensor, q, q, 2.0, ep, ALU.mult, ALU.mult)
            v.reciprocal(inv_scale[:, :], scale).then_inc(S["scale_ready"], 1)

            dve.wait_ge(S["params_T"], 1)
            v.tensor_copy(par[:, 2:4, :], psA[:, 0:2 * H].rearrange("p (k h) -> p k h", h=H)).then_inc(S["par_ready"], 1)
            tau, tw = par[:, 3, :], tau32[:, 0, :]
            dve.wait_ge(S["par_ready"], 1)
            par_step(v.tensor_scalar, tau32[:, 1, :], tau, 32.0, ROUND, ALU.mult, ALU.add)
            v.tensor_tensor(tV[:, :, :], tau.unsqueeze(2).to_broadcast([P, H, RS]),
                            ramp[:, 0:RS].unsqueeze(1).to_broadcast([P, H, RS]), ALU.mult).then_inc(S["thr_chain"], 1)
            n["thr_chain"] += 1
            par_step(v.tensor_scalar, tau32[:, 1, :], tau32[:, 1, :], ROUND, None, ALU.subtract)
            thr_step(v.tensor_scalar, fV[:, :, :], tV[:, :, :], phase[:, 0:1], ROUND, ALU.add, ALU.add)
            par_step(v.scalar_tensor_tensor, tw, tau, 32.0, tau32[:, 1, :], ALU.mult, ALU.subtract)
            par_step(v.tensor_tensor, tU[:, :, :], tw.unsqueeze(2).to_broadcast([P, H, AS]),
                     ramp[:, 0:AS].unsqueeze(1).to_broadcast([P, H, AS]), ALU.mult)
            par_step(v.tensor_scalar, fU[:, 0, :, :], tU[:, :, :], 0.25, ROUND, ALU.add, ALU.add)
            v.tensor_scalar(fU[:, 1, :, :], tU[:, :, :], ROUND, None, ALU.add).then_inc(S["par_chain"], 1)
            dve.wait_ge(S["par_chain"], n["par_chain"])
            v.scalar_tensor_tensor(fU[:, 0, :, :], fU[:, 0, :, :], ROUND, tU[:, :, :], ALU.subtract, ALU.subtract).then_inc(S["sinU_in"], 1)
            n["par_chain"] += 1
            dve.wait_ge(S["par_chain"], n["par_chain"])
            v.scalar_tensor_tensor(fU[:, 1, :, :], fU[:, 1, :, :], ROUND, tU[:, :, :], ALU.subtract, ALU.subtract).then_inc(S["sinU_in"], 1)
            dve.wait_ge(S["thr_chain"], n["thr_chain"])
            v.scalar_tensor_tensor(fV[:, :, :], fV[:, :, :], ROUND, tV[:, :, :], ALU.subtract, ALU.subtract).then_inc(S["sinV_in"], 1)

            dve.wait_ge(S["trig_done"], 2)
            a2, b2, inv = (pm[:, i, :] for i in (8, 9, 10))
            v.tensor_tensor(pm[:, 14, :], em, q, ALU.subtract)
            v.tensor_tensor(a2, aa, aa, ALU.mult)
            v.tensor_tensor(b2, bb, bb, ALU.mult)
            par_step(v.tensor_tensor, pm[:, 15, :], ep, s1, ALU.mult)
            par_step(v.tensor_tensor, a2, a2, b2, ALU.add)
            E = pm[:, 14:16, :]
            aE, bE, G, c0G, c1G = pm[:, 16:18, :], pm[:, 18:20, :], pm[:, 20:22, :], pm[:, 22:24, :], pm[:, 0:2, :]
            a_b = aa.unsqueeze(1).to_broadcast([H, 2, N])
            b_b = bb.unsqueeze(1).to_broadcast([H, 2, N])
            v.tensor_tensor(aE, E, a_b, ALU.mult)
            par_step(v.tensor_tensor, bE, E, b_b, ALU.mult)
            par_step(v.reciprocal, inv, a2)
            v.tensor_tensor(pm[:, 20, :], pm[:, 19, :], pm[:, 16, :], ALU.subtract)
            par_step(v.tensor_tensor, pm[:, 21, :], pm[:, 18, :], pm[:, 17, :], ALU.add)
            par_step(v.scalar_tensor_tensor, G, G, 2.0, inv.unsqueeze(1).to_broadcast([H, 2, N]), ALU.mult, ALU.mult)
            dve.wait_ge(S["in_c"], 16)
            c0 = cin[0:H, :, 0].unsqueeze(1).to_broadcast([H, 2, N])
            c1 = cin[0:H, :, 1].unsqueeze(1).to_broadcast([H, 2, N])
            dve.wait_ge(S["par_chain"], n["par_chain"])
            v.tensor_tensor(c0G, G, c0, ALU.mult)
            par_step(v.tensor_tensor, c1G, G, c1, ALU.mult)
            dve.wait_ge(S["par_chain"], n["par_chain"])
            v.tensor_tensor(pp[:, 0, N:], pm[:, 23, :], pm[:, 0, :], ALU.subtract)
            v.tensor_tensor(pp[:, 1, 0:N], pm[:, 23, :], pm[:, 0, :], ALU.subtract)
            par_step(v.tensor_tensor, pp[:, 0, 0:N], pm[:, 22, :], pm[:, 1, :], ALU.add)
            dve.wait_ge(S["par_chain"], n["par_chain"])
            v.tensor_scalar(pp[:, 1, N:], pp[:, 0, 0:N], -1.0, None, ALU.mult).then_inc(S["params"], 1)

            v.tensor_reduce(own[:, :], ident[:, :].rearrange("p (h b) -> p b h", b=GB), AX_X, ALU.add).then_inc(S["par_chain"], 1)
            n["par_chain"] += 1
            dve.wait_ge(S["masks"], 1)
            par_step(v.reciprocal, linv[:, :], lenf[:, 1, :])
            par_step(v.tensor_tensor, lown[:, :, :], linv[:, :].rearrange("p (g b) -> p g b", b=GB),
                     own[:, :].unsqueeze(1).to_broadcast([P, NG, GB]), ALU.mult)
            par_step(v.tensor_reduce, linv_own[:, :], lown[:, :, :], AX_X, ALU.add)

            dve.wait_ge(S["params_T"], 2)
            par_step(v.tensor_copy, par[:, 0:2, :], psC[3][:, 0:2 * H].rearrange("p (k h) -> p k h", h=H))
            dve.wait_ge(S["sin_done"], 3)
            dve.wait_ge(S["mags"], 1)
            for k in range(2):
                hs = slice(k * H // 2, (k + 1) * H // 2)
                al = par[:, 0, hs].unsqueeze(2).to_broadcast([P, H // 2, AS])
                be = par[:, 1, hs].unsqueeze(2).to_broadcast([P, H // 2, AS])
                par_step(v.tensor_tensor, sU[:, 0, hs, :], sU[:, 0, hs, :], al, ALU.mult)
                v.tensor_tensor(sV[:, hs, :], sV[:, hs, :], magV[:, hs, :], ALU.mult).then_inc(S["kfac"], 1)
                par_step(v.tensor_tensor, sU[:, 1, hs, :], sU[:, 1, hs, :], be, ALU.mult)
                par_step(v.tensor_tensor, sU[:, 0, hs, :], sU[:, 0, hs, :], sU[:, 1, hs, :], ALU.add)
                dve.wait_ge(S["par_chain"], n["par_chain"])
                v.tensor_tensor(tU[:, hs, ::-1], sU[:, 0, hs, :], magU[:, hs, :], ALU.mult).then_inc(S["kfac"], 1)

            m = [0]

            def link(ins):
                m[0] += 1
                ins.then_inc(S["dve_chain"], 1)
                dve.wait_ge(S["dve_chain"], m[0])

            v.tensor_copy(quant[:, :, :], cb[:, 0:1].unsqueeze(2).to_broadcast([P, 4, L]))
            dve.wait_ge(S["slot_done"], 1)
            link(v.tensor_copy(slots[:, :, :], psX[0][:, 0:128].rearrange("p (k j) -> p k j", k=2)))
            link(v.tensor_tensor(slots[:, 0, :], slots[:, 0, :], over[:, :], ALU.add))
            dve.wait_ge(S["norm_ready"], 4)
            for j in range(FAST_SLOTS):
                link(v.tensor_scalar(msk[:, :, :], nrm[:, :, :], slots[:, 0, j:j + 1], None, ALU.is_gt))
                link(v.copy_predicated(quant[:, :, :], msk[:, :, :],
                                       slots[:, 1, j:j + 1].unsqueeze(2).to_broadcast([P, 4, L])))
            n_slots = dve.value_load(n_int[0:1, 0:1], min_val=1, max_val=NTH)
            with dve.If(n_slots > FAST_SLOTS):
                with dve.Fori(FAST_SLOTS, NTH) as j:
                    v.tensor_copy(cur[:, 0:2], slots[:, :, bass.ds(j, 1)].rearrange("p a b -> p (a b)")).then_inc(S["dve_loop"], 1)
                    dve.wait_ge(S["dve_loop"], j * 3 - (3 * FAST_SLOTS - 1))
                    v.tensor_scalar(msk[:, :, :], nrm[:, :, :], cur[:, 0:1], None, ALU.is_gt).then_inc(S["dve_loop"], 1)
                    dve.wait_ge(S["dve_loop"], j * 3 - (3 * FAST_SLOTS - 2))
                    v.tensor_copy(cur[:, 2:3], cur[:, 0:1])
                    v.copy_predicated(quant[:, :, :], msk[:, :, :],
                                      cur[:, 1:2].unsqueeze(2).to_broadcast([P, 4, L])).then_inc(S["dve_loop"], 1)
                    dve.wait_ge(S["dve_loop"], j * 3 - (3 * FAST_SLOTS - 3))

            def weff(t):
                q, m = quant[:, t, :], nrm[:, t, :]
                link(v.tensor_tensor(q, q, m, ALU.subtract))
                link(v.tensor_tensor(q, q, m, ALU.add))
                q3 = q.rearrange("p (g k) -> p g k", k=P)
                link(v.tensor_tensor(q3, q3, scale[:, 4 * t:4 * t + 4].unsqueeze(2).to_broadcast([P, 4, P]), ALU.mult))
                link(v.tensor_tensor(q, q, dlt[:, t, :], ALU.add))
                qd = q[:, t * P:(t + 1) * P]
                v.tensor_tensor(qd, qd, ident[:, :], ALU.add).then_inc(S["weff"], 1)

            def add_halves(i):
                dve.wait_ge(S["mhalf_ready"], i + 1)
                h2 = mhalf[:, i % 4, :].rearrange("p (k g n) -> p k g n", k=2, g=NG)
                dst = msum[:, :, 2 * i * GB:(2 * i + 2) * GB]
                v.tensor_tensor(dst, h2[:, 0], h2[:, 1], ALU.add).then_inc(S["mhalf_used"], 1)

            dve.wait_ge(S["xt_sb"], NG)
            for i in range(NPAIR):
                dve.wait_ge(S["conv_done"], i + 1)
                dst = xT[:, :, :, 2 * i:2 * i + 2, :].rearrange("p c g h b -> p h (c g) b")
                kp = keep[:, :, :].rearrange("p c (g b) -> p (c g) b", b=GB).unsqueeze(1).to_broadcast([P, 2, NC * NG, GB])
                v.copy_predicated(dst, kp, psC[i % 4][:, :].rearrange("p (h n b) -> p h n b", h=2, b=GB)
                                  ).then_inc(S["conv_used"], 1)
                if i >= 3:
                    add_halves(i - 3)
                if i in (1, 3, 5, 7):
                    weff(i // 2)
                if i == 9:
                    dve.wait_ge(S["sel_loaded"], 16 * GB)
                    link(v.tensor_tensor(gmat[:, :, :].rearrange("p g (d b) -> p (g d) b", b=GB),
                                         wrows[:, :, :].rearrange("p g d -> p (g d)").unsqueeze(2).to_broadcast([P, NG * H, GB]),
                                         own[:, :].unsqueeze(1).to_broadcast([P, NG * H, GB]), ALU.mult))
                if i == 11:
                    link(v.tensor_tensor(gmat[:, :, :], gmat[:, :, :], ident[:, :].unsqueeze(1).to_broadcast([P, NG, P]), ALU.add))
            for i in range(NPAIR - 3, NPAIR):
                add_halves(i)
            dve.wait_ge(S["ymean"], 1)
            v.tensor_tensor(gmean[:, :], psA[:, 0:NG], linv_own[:, :], ALU.mult).then_inc(S["gmean_ready"], 1)
            dve.wait_ge(S["gate_th"], 1)
            link(v.tensor_scalar(gate[:, :], gth[:, :], 0.5, 1.5, ALU.mult, ALU.add))
            v.tensor_tensor(gmat[:, :, :], gmat[:, :, :], gate[:, :].unsqueeze(2).to_broadcast([P, NG, P]), ALU.mult).then_inc(S["gated"], 1)
            for g in range(NG):
                dve.wait_ge(S["o_done"], g + 1)
                if g >= 4:
                    dve.wait_ge(stored[g % 4], 16 * (g // 4))
                v.tensor_copy(osb[:, g % 4, :], psX[g % 2][:, :]).then_inc(S["o_sb"], 1)

        @block.tensor
        def _(pe):
            m = nc.tensor
            pe.wait_ge(S["consts"], 1)
            pe.wait_ge(S["in_lb"], 16)
            for t in range(4):
                last = m.transpose(psB[0:R, t * P:(t + 1) * P], lb[:, t, :], ident[:, :])
            last.then_inc(S["lbT_done"], 1)
            pe.wait_ge(S["in_la"], 16)
            pe.wait_ge(S["lbT_sb"], 1)
            for t in range(4):
                m.matmul(psC[t][:, :], lbT[:, t * P:(t + 1) * P], la[:, :], start=True, stop=True).then_inc(S["delta_done"], 1)
            pe.wait_ge(S["sel_oh"], 1)
            pe.wait_ge(S["in_wall"], 16)
            for i in range(2):
                m.matmul(psX[i][0:B, :], onehot[:, :], wall[:, i * 512:(i + 1) * 512], start=True, stop=True).then_inc(S["sel_done"], 1)

            def x_transposes(g):
                pe.wait_ge(in_x[g], 16)
                if g >= 2:
                    pe.wait_ge(S["xt_sb"], g - 1)
                else:
                    pe.wait_ge(S["sel_sb"], g + 1)
                for c in range(NC):
                    last = m.transpose(psX[g % 2][:, c * P:(c + 1) * P], xrows[:, g, c * P:(c + 1) * P], ident[:, :])
                last.then_inc(S["xt_done"], 1)

            def param_transposes(k0, bank, n):
                pe.wait_ge(S["params"], n)
                for k in range(k0, k0 + 2):
                    last = m.transpose(bank[:, (k - k0) * H:(k - k0 + 1) * H], pp[:, k, :], ident[0:H, 0:H])
                last.then_inc(S["params_T"], 1)

            param_transposes(2, psA, 1)
            for g in range(NG):
                x_transposes(g)
                if g == 11:
                    pe.wait_ge(S["delta_sb"], 4)
                    param_transposes(0, psC[3], 2)
            pe.wait_ge(S["slot_ready"], 1)
            pe.wait_ge(S["xt_sb"], NG)
            m.matmul(psX[0][:, 0:128], ones[0:NTH, :], slot_rhs[0:NTH, :, :].rearrange("p k j -> p (k j)"),
                     start=True, stop=True).then_inc(S["slot_done"], 1)
            pe.wait_ge(S["drow_ready"], 1)
            pe.wait_ge(S["par_ready"], 1)
            for k, bank in ((0, psA), (1, psB)):
                m.matmul(bank[0:AS, :], last_a[0:1, :], drow[:, k * H // 2:(k + 1) * H // 2, :].rearrange("p h r -> p (h r)"),
                         start=True, stop=False, skip_group_check=True)
            for k, bank in ((0, psA), (1, psB)):
                pe.wait_ge(S["kfac"], 2 * k + 2)
                for j in range(H // 2):
                    h = k * H // 2 + j
                    last = m.matmul(bank[0:AS, j * RS:(j + 1) * RS], tU[:, h, :], sV[:, h, :],
                                    start=False, stop=True, skip_group_check=True)
                last.then_inc(S["k_done"], 1)

            def weff_transposes(c):
                if c == 0:
                    pe.wait_ge(S["weff"], 4)
                if c >= 2:
                    pe.wait_ge(S["wT_sb"], c - 1)
                for t in range(4):
                    last = m.transpose(psX[c % 2][:, t * P:(t + 1) * P], quant[:, t, c * P:(c + 1) * P], ident[:, :])
                last.then_inc(S["wT_done"], 1)

            pe.wait_ge(S["xt_sb"], NG)
            for i in range(NPAIR):
                pe.wait_ge(S["turned"], i + 1)
                if i >= 4:
                    pe.wait_ge(S["conv_used"], i - 3)
                for j in range(2):
                    h = 2 * i + j
                    xh = xT[:, :, :, h, :].rearrange("p c g b -> p (c g) b")
                    for d in range(NC):
                        n = (NC - d) * B
                        o = j * NC * B + d * B
                        last = m.matmul(psC[i % 4][:, o:o + n], toep[:, i % NSLOT, j, d * P:(d + 1) * P], xh[:, 0:n // GB, :],
                                        start=(d == 0), stop=(d == NC - 1), skip_group_check=True)
                last.then_inc(S["conv_done"], 1)
                if 11 <= i < 15:
                    weff_transposes(i - 11)

            def rows(g, c):
                return xT[:, c, g, :, :].rearrange("p h b -> p (h b)")

            pe.wait_ge(S["conv_used"], NPAIR)
            pe.wait_ge(S["wT_sb"], NC)

            def mean(g):
                m_ = m.matmul(psA[:, g:g + 1], msum[:, g, :], ones[:, 0:1],
                              start=True, stop=True, skip_group_check=True)
                if g == NG - 1:
                    m_.then_inc(S["ymean"], 1)

            def times_m(g):
                if g >= 4:
                    pe.wait_ge(S["y_sb"], g - 3)
                for c in range(NC):
                    last = m.matmul(psC[g % 4][:, :], rows(g, c), mt[:, c, :], start=(c == 0), stop=(c == NC - 1))
                    if g in (1, 2):
                        for k in range(2):
                            mean(8 * (g - 1) + 2 * c + k)
                last.then_inc(S["y_done"], 1)

            def mix(g):
                pe.wait_ge(S["y_sb"], g + 1)
                if g >= 2:
                    pe.wait_ge(S["o_sb"], g - 1)
                m.matmul(psX[g % 2][:, :], gmat[:, g, :], ysb[:, g % 8, :], start=True, stop=True).then_inc(S["o_done"], 1)

            for g in range(NG):
                if g == 1:
                    pe.wait_ge(S["mhalf_used"], NPAIR)
                times_m(g)
                if g == 3:
                    pe.wait_ge(S["gmean_ready"], 1)
                    pe.wait_ge(S["cmat_ready"], 1)
                    m.matmul(psB[:, 0:NG], cmat[:, :], gmean[:, :], start=True, stop=True).then_inc(S["chan"], 1)
                if g == MIX_LAG:
                    pe.wait_ge(S["gated"], 1)
                if g >= MIX_LAG:
                    mix(g - MIX_LAG)
            for g in range(NG - MIX_LAG, NG):
                mix(g)


_INS = ['x', 'itok_B_78_3631', 'itok_B_9_3973', 'condB_codebook', 'itok_B_0_15', 'L0_cond_log_dt', 'L0_cond_C',
        'L0_cond_log_A_real', 'L0_cond_A_imag', 'L0_cond_D', 'L1_cond_conv_w', 'L2_cond_weight', 'L2_cond_scale_log',
        'L2_cond_lora_A', 'L2_cond_lora_B', 'L3_cond_weights']
_OUTS = [((64, 32, 512), 'float32')]


def kernel(**inputs):
    import numpy as _np
    import concourse.bacc as _bacc
    from concourse import mybir as _mybir
    from concourse.bass_utils import run_bass_kernel_spmd as _run

    nc = _bacc.Bacc("TRN2", target_bir_lowering=False, num_devices=1)
    arrays, args = {}, []
    for name in _INS:
        a = _np.ascontiguousarray(inputs[name])
        arrays[f"in_{name}_dram"] = a
        args.append(nc.dram_tensor(f"in_{name}_dram", a.shape, _mybir.dt.from_np(a.dtype), kind="ExternalInput").ap())
    for i, (shape, dtype) in enumerate(_OUTS):
        dt = _mybir.dt.from_np(_np.dtype(dtype))
        args.append(nc.dram_tensor(f"out_{i}_dram", shape, dt, kind="ExternalOutput").ap())
    cond_resid_kernel(nc, *args)
    r = _run(nc, [arrays], core_ids=[0])
    got = tuple(r.results[0][f"out_{i}_dram"] for i in range(len(_OUTS)))
    return got[0]
```

```python
from contextlib import ExitStack

import concourse.bass as bass
from concourse import mybir

ALU = mybir.AluOpType
ACT = mybir.ActivationFunctionType
F32 = mybir.dt.float32
I32 = mybir.dt.int32
F32R = mybir.dt.float32r
AX_X = mybir.AxisListType.X

P = 128
TWO_PI = 6.2831850
ROUND = 12582912.0
BIG = 3.0e38
LN2_HI, LN2_LO = 0.693359375, -2.12194440e-4
PI2_A, PI2_B, PI2_C = 6.28125, 1.9350051879882812e-3, 3.0199159819e-7
MIX_LAG = 3
X_BEFORE_K, T2_AT, SIN_AT = 8, 5, 2
FAST_SLOTS = 4


def cond_resid_kernel(nc, x, len_conv, len_gate, codebook, cond, log_dt, C, log_A_real, A_imag, D, conv_w,
                      weight, scale_log, lora_A, lora_B, cond_W, out):
    B, H, L = x.shape
    N = A_imag.shape[1]
    NC = L // P
    GB = P // H
    NG = B // GB
    NPAIR = H // 2
    NCODE = codebook.shape[0]
    NTH = NCODE - 1
    R = lora_A.shape[0]
    NK = cond_W.shape[0]
    TAPS = conv_w.shape[2]
    AS, RS = L // 32, 32
    NSLOT = 3
    PAD = L + P

    with ExitStack() as ctx:
        def sb(name, shape, dt=F32):
            return ctx.enter_context(nc.sbuf_tensor(name, shape, dt))

        def spent(name, shape, dt=F32):
            with nc.sbuf_tensor(name, shape, dt) as buffer:
                return buffer

        def sem(name):
            return ctx.enter_context(nc.semaphore(name))

        psX = [ctx.enter_context(nc.psum_tensor(f"psX{i}", [P, 512], F32)) for i in range(2)]
        psA = ctx.enter_context(nc.psum_tensor("psA", [P, 512], F32))
        psB = ctx.enter_context(nc.psum_tensor("psB", [P, 512], F32))
        psC = [ctx.enter_context(nc.psum_tensor(f"psC{i}", [P, 512], F32)) for i in range(4)]

        kpad = nc.dram_tensor("kpad", [H, PAD], F32, kind="Internal")
        wsel_dram = nc.dram_tensor("wsel_dram", [B, H * H], F32, kind="Internal")

        xrows = spent("xrows", [P, NG, L])
        x_hi = sb("x_hi", [P, NC, NG, H, GB], F32R)
        w_in = sb("w_in", [P, 4, L])
        la = sb("la", [R, L])
        lb = sb("lb", [P, 4, R])
        lns = sb("lns", [P, 1 + N + 16])
        bim = sb("bim", [P, N])
        cin = sb("cin", [P, N, 2])
        drow = sb("drow", [1, H, RS])
        dcol = sb("dcol", [1, H])
        last_a = sb("last_a", [P, AS])
        cb = sb("cb", [P, NCODE])
        cwt = sb("cwt", [P, TAPS])
        leni = sb("leni", [P, 2, B], I32)
        condi = sb("condi", [NK, B], I32)
        wall = sb("wall", [NK, H * H])

        diff = sb("diff", [P, P])
        ident = sb("ident", [P, P])
        tri = sb("tri", [P, P])
        own = sb("own", [P, GB])
        pcol = sb("pcol", [P, 1])
        ramp = sb("ramp", [P, 64])
        ramp1 = sb("ramp1", [P, 64])
        phase = sb("phase", [P, 1])
        phase_rad = sb("phase_rad", [P, 1])
        quarter_rad = sb("quarter_rad", [P, 1])
        ones = sb("ones", [P, P])
        zpad = sb("zpad", [H, P])

        ex = sb("ex", [P, 6, 1 + N + 16])
        exi = sb("exi", [P, 1 + N + 16], I32)
        pm = sb("pm", [H, 24, N])
        pp = sb("pp", [H, 4, 2 * N])
        par = sb("par", [P, 4, H])
        sq = sb("sq", [P, 8, H])
        magV = sb("magV", [P, H, RS])
        magU = sb("magU", [P, H, AS])
        tau32 = sb("tau32", [P, 2, H])
        tV = sb("tV", [P, H, RS])
        tU = sb("tU", [P, H, AS])
        fV = sb("fV", [P, H, RS])
        fU = sb("fU", [P, 2, H, AS])
        sV, sU = fV, fU
        ksb = sb("ksb", [AS, H, RS])

        th = sb("th", [P, 64])
        tp = sb("tp", [P, 65])
        act_row = sb("act_row", [P, 64])
        scr = sb("scr", [P, 4, 64])
        small = sb("small", [P, 16])
        slot_rhs = sb("slot_rhs", [64, 2, 64])
        slots = sb("slots", [P, 2, 64])
        over = sb("over", [P, 64])
        n_int = sb("n_int", [P, 1], I32)
        cur = sb("cur", [P, 3])
        inv_scale = sb("inv_scale", [P, 16])
        lbT = sb("lbT", [R, L])
        dlt = spent("dlt", [P, 4, L])
        g_hi = sb("g_hi", [P, NG, P], F32R)
        nrm = spent("nrm", [P, 4, L])
        mt_lo = sb("mt_lo", [P, NC, L], F32R)
        msk = spent("msk", [P, 4, L], I32)
        mt_hi = sb("mt_hi", [P, NC, L], F32R)
        quant = sb("quant", [P, 4, L])

        lenf = sb("lenf", [P, 2, B])
        keep = sb("keep", [P, NC, B], I32)
        mask2 = sb("mask2", [P, NC, B])
        linv = sb("linv", [P, B])
        xT = spent("xT", [P, NC, NG, H, GB])
        x_lo = sb("x_lo", [P, NC, NG, H, GB], F32R)
        with nc.sbuf_tensor("toep", [P, NSLOT, 2, L], F32) as toep:
            hank = spent("hank", [P, NSLOT, 2, L])
        y_hi = sb("y_hi", [P, 4, L], F32R)
        y_lo = sb("y_lo", [P, 4, L], F32R)
        osb = sb("osb", [P, 4, L])
        cmat = sb("cmat", [P, P])
        ctmp = sb("ctmp", [P, P])
        lown = sb("lown", [P, NG, GB])
        linv_own = sb("linv_own", [P, NG])
        mtmp = fU[:, 0, :, :].rearrange("p h a -> p (h a)")
        mhalf = tV[:, :, :].rearrange("p h r -> p (h r)").rearrange("p (s n) -> p s n", s=4)
        msum = w_in[:, :, :].rearrange("p t i -> p (t i)").rearrange("p (g n) -> p g n", g=NG)
        gmean = sb("gmean", [P, NG])
        gth = sb("gth", [P, NG])
        gate = sb("gate", [P, NG])
        condf = sb("condf", [NK, B])
        onehot = sb("onehot", [NK, B])
        wsel = sb("wsel", [B, H * H])
        wrows = sb("wrows", [P, NG, H])
        gmat = spent("gmat", [P, NG, P])
        g_lo = sb("g_lo", [P, NG, P], F32R)

        S = {n: sem(n) for n in (
            "in_lns in_imag in_c in_d in_cb in_cw in_len in_cond in_w in_la in_lb in_wall "
            "consts pool_chain par_chain thr_chain dve_chain dve_loop "
            "drow_ready pad_written k_written tanh_in tanh_done trig_in trig_done params params_T par_ready mags "
            "sinV_in sinU_in sin_done kfac kfac_v k_done ksb_ready scale_ready raw_ready "
            "lbT_done lbT_sb delta_done delta_sb sel_oh sel_done sel_sb sel_written sel_loaded "
            "xt_done xt_sb slot_ready slot_done turned conv_done conv_used mhalf_ready mhalf_used msum_ready "
            "weff wT_done mt_hi_sb mt_lo_sb masks own_ready slots_sb masked gmat_ready g_hi_ready g_lo_ready hi_ready lo_ready cmat_ready ymean gmean_ready chan gate_th gated y_hi_sb "
            "y_done y_sb o_done o_sb").split()}
        k_written = [sem(f"k_written{i}") for i in range(2)]
        in_x = [sem(f"in_x{i}") for i in range(NG)]
        in_hank = [sem(f"in_hank{i}") for i in range(NSLOT)]
        stored = [sem(f"stored{i}") for i in range(4)]

        x_rows = x.rearrange("(g b) h l -> g h b l", b=GB)
        o_rows = out.rearrange("(g b) h l -> g h b l", b=GB)

        def hankel_rows(i):
            return bass.AP(kpad, 2 * i * PAD, [[1, P], [PAD, 2], [1, L]])

        block = ctx.enter_context(nc.Block())

        @block.sync
        def _(sp):
            sp.dma_start(lns[:, 1:1 + N], bass.AP(log_A_real.tensor, 0, [[0, GB], [N, H], [1, N]])).then_inc(S["in_lns"], 16)
            sp.dma_start(lns[:, 0:1], bass.AP(log_dt.tensor, 0, [[0, GB], [1, H], [1, 1]])).then_inc(S["in_lns"], 16)
            sp.dma_start(lns[:, 1 + N:].rearrange("p (t g) -> p t g", t=4),
                         scale_log.rearrange("(t p) g k -> p t (g k)", p=P)).then_inc(S["in_lns"], 16)
            sp.dma_start(bim[:, :], bass.AP(A_imag.tensor, 0, [[0, GB], [N, H], [1, N]])).then_inc(S["in_imag"], 16)
            sp.dma_start(cin[:, :, :], bass.AP(C.tensor, 0, [[0, GB], [2 * N, H], [2, N], [1, 2]])).then_inc(S["in_c"], 16)
            sp.dma_start(condi[:, :], bass.AP(cond.tensor, 0, [[0, NK], [1, B]])).then_inc(S["in_cond"], 16)
            sp.dma_start(wall[:, :], cond_W.rearrange("k c d -> k (c d)")).then_inc(S["in_wall"], 16)
            sp.dma_start(leni[:, 0, :], bass.AP(len_conv.tensor, 0, [[0, P], [1, B]])).then_inc(S["in_len"], 16)
            sp.dma_start(leni[:, 1, :], bass.AP(len_gate.tensor, 0, [[0, P], [1, B]])).then_inc(S["in_len"], 16)
            sp.dma_start(dcol[:, :], D.rearrange("(o h) -> o h", o=1)).then_inc(S["in_d"], 16)
            for g in range(NG):
                sp.dma_start(xrows[:, g, :], x_rows[g]).then_inc(in_x[g], 16)
                if g == 3:
                    sp.dma_start(w_in[:, :, :], weight.rearrange("(t p) i -> p t i", p=P)).then_inc(S["in_w"], 16)
                if g == 5:
                    sp.dma_start(cwt[:, :], bass.AP(conv_w.tensor, 0, [[0, P], [1, TAPS]])).then_inc(S["in_cw"], 16)
            sp.wait_ge(S["consts"], 1)
            sp.dma_start(kpad[:, L:PAD], zpad[:, :]).then_inc(S["pad_written"], 16)
            sp.wait_ge(S["sel_sb"], 2)
            sp.dma_start(wsel_dram[:, :], wsel[:, :]).then_inc(S["sel_written"], 16)
            sp.wait_ge(S["sel_written"], 16)
            for b in range(GB):
                sp.dma_start(wrows[b:P:GB, :, :], bass.AP(wsel_dram, b * H * H, [[H, H], [GB * H * H, NG], [1, H]])
                             ).then_inc(S["sel_loaded"], 16)
            sp.wait_ge(S["pad_written"], 16)
            for i in range(NPAIR):
                if i % (NPAIR // 2) == 0:
                    sp.wait_ge(k_written[i // (NPAIR // 2)], 16)
                if i >= NSLOT:
                    sp.wait_ge(S["turned"], i - NSLOT + 1)
                sp.dma_start(hank[:, i % NSLOT, :, :], hankel_rows(i)).then_inc(in_hank[i % NSLOT], 16)
            for g in range(NG):
                sp.wait_ge(S["o_sb"], g + 1)
                sp.dma_start(o_rows[g], osb[:, g % 4, :]).then_inc(stored[g % 4], 16)
            for i in range(4):
                sp.wait_ge(stored[i], 16 * (NG // 4))

        @block.gpsimd
        def _(pool):
            n = [0]

            def link(ins):
                n[0] += 1
                ins.then_inc(S["pool_chain"], 1)
                pool.wait_ge(S["pool_chain"], n[0])

            g = nc.gpsimd
            g.iota(diff[:, :], [[1, P]], base=0, channel_multiplier=-1, allow_small_or_imprecise_dtypes=True)
            g.iota(pcol[:, :], [[0, 1]], base=0, channel_multiplier=1, allow_small_or_imprecise_dtypes=True)
            g.iota(ramp[:, :], [[1, 64]], base=0, channel_multiplier=0, allow_small_or_imprecise_dtypes=True)
            link(g.iota(ramp1[:, :], [[1, 64]], base=1, channel_multiplier=0, allow_small_or_imprecise_dtypes=True))
            g.tensor_scalar(tri[:, :], diff[:, :], 0.0, None, ALU.is_le)
            g.tensor_scalar(ident[:, :], diff[:, :], 0.0, None, ALU.is_equal)
            g.memset(zpad[:, :], 0.0)
            g.memset(ones[:, :], 1.0)
            g.memset(quarter_rad[:, :], 0.25 * TWO_PI)
            g.tensor_scalar(phase[:, :], pcol[:, :], float(N), 0.25, ALU.is_lt, ALU.mult)
            g.tensor_scalar(phase_rad[:, :], pcol[:, :], float(N), 0.25 * TWO_PI, ALU.is_lt, ALU.mult)
            g.tensor_scalar(last_a[:, :], ramp[:, 0:AS], float(AS - 1), None, ALU.is_equal).then_inc(S["consts"], 1)
            link(g.memset(drow[:, :, :], 0.0))
            pool.wait_ge(S["in_d"], 16)
            g.tensor_scalar(drow[:, :, 0], dcol[:, :], 1.0, None, ALU.add).then_inc(S["drow_ready"], 1)
            pool.wait_ge(S["in_cond"], 16)
            link(g.tensor_copy(condf[:, :], condi[:, :]))
            g.tensor_scalar(onehot[:, :], condf[:, :], pcol[0:NK, 0:1], None, ALU.is_equal).then_inc(S["sel_oh"], 1)
            pool.wait_ge(S["in_len"], 32)
            link(g.tensor_copy(lenf[:, :, :], leni[:, :, :]))
            for c in range(NC):
                g.tensor_scalar(keep[:, c, :], lenf[:, 0, :], pcol[:, 0:1], float(P * c), ALU.subtract, ALU.is_gt)
                last = g.tensor_scalar(mask2[:, c, :], lenf[:, 1, :], pcol[:, 0:1], float(P * c), ALU.subtract, ALU.is_gt)
            last.then_inc(S["masks"], 1)

            link(g.memset(magV[:, :, 0:1], 1.0))
            link(g.memset(magU[:, :, 0:1], 1.0))
            pool.wait_ge(S["par_ready"], 1)
            pows = [par[:, 2, :]]
            for k in range(8):
                link(g.tensor_tensor(sq[:, k, :], pows[k], pows[k], ALU.mult))
                pows.append(sq[:, k, :])
            for k in range(4):
                w = 1 << k
                link(g.tensor_tensor(magU[:, :, w:2 * w], magU[:, :, 0:w],
                                     pows[5 + k].unsqueeze(2).to_broadcast([P, H, w]), ALU.mult))
            for k in range(5):
                w = 1 << k
                last = g.tensor_tensor(magV[:, :, w:2 * w], magV[:, :, 0:w],
                                       pows[k].unsqueeze(2).to_broadcast([P, H, w]), ALU.mult)
                if k < 4:
                    link(last)
            last.then_inc(S["mags"], 1)
            pool.wait_ge(S["sin_done"], 3)
            pool.wait_ge(S["mags"], 1)
            for k in range(2):
                hs = slice(k * H // 2, (k + 1) * H // 2)
                g.tensor_tensor(sV[:, hs, :], sV[:, hs, :], magV[:, hs, :], ALU.mult).then_inc(S["kfac_v"], 1)
            pool.wait_ge(S["in_w"], 16)
            pool.wait_ge(S["delta_sb"], 4)
            for t in range(4):
                g.tensor_tensor(w_in[:, t, :], w_in[:, t, :], dlt[:, t, :], ALU.add).then_inc(S["raw_ready"], 1)
            pool.wait_ge(S["own_ready"], 1)
            pool.wait_ge(S["sel_loaded"], 16 * GB)
            link(g.tensor_tensor(gmat[:, :, :].rearrange("p g (d b) -> p (g d) b", b=GB),
                                 wrows[:, :, :].rearrange("p g d -> p (g d)").unsqueeze(2).to_broadcast([P, NG * H, GB]),
                                 own[:, :].unsqueeze(1).to_broadcast([P, NG * H, GB]), ALU.mult))
            g.tensor_tensor(gmat[:, :, :], gmat[:, :, :], ident[:, :].unsqueeze(1).to_broadcast([P, NG, P]), ALU.add
                            ).then_inc(S["gmat_ready"], 1)
            pool.wait_ge(S["in_cw"], 16)
            for k in range(TAPS):
                link(g.tensor_scalar(ctmp[:, :], diff[:, :], float(GB * (TAPS // 2 - k)), cwt[:, k:k + 1], ALU.is_equal, ALU.mult))
                if k == 0:
                    link(g.tensor_copy(cmat[:, :], ctmp[:, :]))
                elif k < TAPS - 1:
                    link(g.tensor_tensor(cmat[:, :], cmat[:, :], ctmp[:, :], ALU.add))
                else:
                    g.tensor_tensor(cmat[:, :], cmat[:, :], ctmp[:, :], ALU.add).then_inc(S["cmat_ready"], 1)
            half = NC // 2 * NG * 2 * GB
            for i in range(NPAIR):
                pool.wait_ge(S["conv_used"], i + 1)
                if i > 0:
                    pool.wait_ge(S["mhalf_ready"], i)
                pair = xT[:, :, :, 2 * i:2 * i + 2, :].rearrange("p c g h b -> p (c g) h b")
                g.tensor_tensor(
                    mtmp.rearrange("p (n h b) -> p n h b", h=2, b=GB), pair,
                    mask2[:, :, :].rearrange("p c (g b) -> p (c g) b", b=GB).unsqueeze(2).to_broadcast([P, NC * NG, 2, GB]),
                    ALU.mult).then_inc(S["masked"], 1)
                pool.wait_ge(S["masked"], i + 1)
                if i >= 4:
                    pool.wait_ge(S["mhalf_used"], i - 3)
                g.tensor_tensor(mhalf[:, i % 4, :], mtmp[:, 0:half], mtmp[:, half:], ALU.add).then_inc(S["mhalf_ready"], 1)

        @block.scalar
        def _(act):
            a = nc.scalar
            act.dma_start(cb[:, :], bass.AP(codebook.tensor, 0, [[0, P], [1, NCODE]])).then_inc(S["in_cb"], 16)
            act.dma_start(lb[:, :, :], lora_B.rearrange("(t p) r -> p t r", p=P)).then_inc(S["in_lb"], 16)
            act.dma_start(la[:, :], lora_A).then_inc(S["in_la"], 16)

            def x_evac(g):
                act.wait_ge(S["xt_done"], g + 1)
                dst = xT[:, :, g, :, :].rearrange("p c h b -> p c (h b)")
                a.copy(dst, psX[g % 2][:, :].rearrange("p (c n) -> p c n", c=NC)).then_inc(S["xt_sb"], 1)

            act.wait_ge(S["lbT_done"], 1)
            a.mul(lbT[:, :], psB[0:R, :], 0.5).then_inc(S["lbT_sb"], 1)
            act.wait_ge(S["tanh_in"], 1)
            a.activation(pm[:, 7, :], pm[:, 0, :], ACT.Tanh, scale=0.5).then_inc(S["tanh_done"], 1)
            act.wait_ge(S["trig_in"], 1)
            a.activation(pm[:, 6, :], pm[:, 4, :], ACT.Sin, scale=0.5).then_inc(S["trig_done"], 1)
            a.activation(pm[:, 5, :], pm[:, 4, :], ACT.Sin).then_inc(S["trig_done"], 1)
            def kernels_out(k, bank):
                act.wait_ge(S["k_done"], k + 1)
                hs = slice(k * H // 2, (k + 1) * H // 2)
                a.copy(ksb[:, hs, ::-1], bank[0:AS, :].rearrange("a (h r) -> a h r", r=RS)).then_inc(S["ksb_ready"], 1)
                act.wait_ge(S["ksb_ready"], k + 1)
                act.dma_start(bass.AP(kpad, k * (H // 2) * PAD, [[RS, AS], [PAD, H // 2], [1, RS]]),
                              ksb[:, hs, :]).then_inc(k_written[k], 16)

            def delta_evac(t):
                act.wait_ge(S["delta_done"], t + 1)
                a.copy(dlt[:, t, :], psC[t][:, :]).then_inc(S["delta_sb"], 1)

            delta_evac(0)
            delta_evac(1)
            for i in range(2):
                act.wait_ge(S["sel_done"], i + 1)
                a.copy(wsel[:, i * 512:(i + 1) * 512], psX[i][0:B, :]).then_inc(S["sel_sb"], 1)
            delta_evac(2)
            delta_evac(3)
            act.wait_ge(S["consts"], 1)
            for g in range(NG):
                if g == SIN_AT:
                    act.wait_ge(S["sinU_in"], 1)
                    a.activation(sU[:, 0, :, :], fU[:, 0, :, :], ACT.Sin, bias=quarter_rad[:, 0:1],
                                 scale=-TWO_PI).then_inc(S["sin_done"], 1)
                    act.wait_ge(S["sinU_in"], 2)
                    a.activation(sU[:, 1, :, :], fU[:, 1, :, :], ACT.Sin, scale=-TWO_PI).then_inc(S["sin_done"], 1)
                    act.wait_ge(S["sinV_in"], 1)
                    a.activation(sV[:, :, :], fV[:, :, :], ACT.Sin, bias=phase_rad[:, 0:1],
                                 scale=-TWO_PI).then_inc(S["sin_done"], 1)
                if g == X_BEFORE_K:
                    kernels_out(0, psA)
                    kernels_out(1, psB)
                x_evac(g)

            def upper(i):
                act.wait_ge(S["conv_used"], i + 1)
                a.copy(x_hi[:, :, :, 2 * i:2 * i + 2, :].rearrange("p c g h b -> p (c g) h b"),
                       xT[:, :, :, 2 * i:2 * i + 2, :].rearrange("p c g h b -> p (c g) h b")).then_inc(S["hi_ready"], 1)

            def mt_upper(c):
                act.wait_ge(S["wT_done"], c + 1)
                a.copy(mt_hi[:, c, :], psX[c % 2][:, :]).then_inc(S["mt_hi_sb"], 1)

            for i in range(NPAIR):
                act.wait_ge(in_hank[i % NSLOT], 16 * (i // NSLOT + 1))
                if i >= NSLOT:
                    act.wait_ge(S["conv_done"], i - NSLOT + 1)
                a.copy(toep[:, i % NSLOT, :, :], hank[:, i % NSLOT, :, ::-1]).then_inc(S["turned"], 1)
                if i >= NSLOT:
                    upper(i - NSLOT)
                if 10 <= i < 14:
                    act.wait_ge(S["gmat_ready"], 1)
                    act.wait_ge(S["weff"], 4)
                    q = slice(4 * (i - 10), 4 * (i - 9))
                    a.copy(g_hi[:, q, :], gmat[:, q, :]).then_inc(S["g_hi_ready"], 1)
            for k in range(NSLOT):
                upper(NPAIR - NSLOT + k)
                mt_upper(k)
            mt_upper(3)
            for g in range(NG):
                if g == 0:
                    act.wait_ge(S["chan"], 1)
                    a.activation(gth[:, :], psB[:, 0:NG], ACT.Tanh, scale=0.5).then_inc(S["gate_th"], 1)
                    act.wait_ge(S["gated"], 1)
                act.wait_ge(S["y_done"], g + 1)
                if g >= 4:
                    act.wait_ge(S["o_done"], g - 3)
                a.activation(y_hi[:, g % 4, :], psC[g % 4][:, :], ACT.Copy, scale=gate[:, g:g + 1]).then_inc(S["y_hi_sb"], 1)

        @block.vector
        def _(dve):
            v = nc.vector
            n = {"par_chain": 0, "thr_chain": 0}

            def chained(name):
                def step(op, *args):
                    if n[name]:
                        dve.wait_ge(S[name], n[name])
                    op(*args).then_inc(S[name], 1)
                    n[name] += 1
                return step

            par_step, thr_step = chained("par_chain"), chained("thr_chain")

            mx, mn, cnt, rank, actc, tcol, ccol = (small[:, i:i + 1] for i in range(7))
            v.memset(tp[:, 0:1], -BIG)
            v.memset(tp[:, 64:65], BIG)
            dve.wait_ge(S["in_cb"], 16)
            thr_step(v.tensor_reduce, mx, cb[:, :], AX_X, ALU.max)
            thr_step(v.tensor_reduce, mn, cb[:, :], AX_X, ALU.min)
            thr_step(v.scalar_tensor_tensor, mx, mn, -1.0, mx, ALU.mult, ALU.max)
            thr_step(v.tensor_scalar, mx, mx, 1e-8, None, ALU.max)

            y, k, r, p = (ex[:, i, :] for i in range(4))
            dve.wait_ge(S["in_lns"], 48)
            par_step(v.tensor_scalar, y, lns[:, :], -87.0, 88.0, ALU.max, ALU.min)
            thr_step(v.reciprocal, mx, mx)
            par_step(v.tensor_scalar, k, y, 1.4426950408889634, ROUND, ALU.mult, ALU.add)
            thr_step(v.tensor_scalar, cb[:, :], cb[:, :], mx, None, ALU.mult)
            par_step(v.tensor_scalar, k, k, ROUND, None, ALU.subtract)
            thr_step(v.tensor_tensor, th[:, 1:64], cb[:, 0:NTH], cb[:, 1:NCODE], ALU.add)
            par_step(v.scalar_tensor_tensor, r, k, -LN2_HI, y, ALU.mult, ALU.add)
            thr_step(v.tensor_scalar, th[:, 1:64], th[:, 1:64], 0.5, None, ALU.mult)
            par_step(v.scalar_tensor_tensor, r, k, -LN2_LO, r, ALU.mult, ALU.add)

            def tree(level):
                s = 32 >> level
                return tp[:, s:64:2 * s], th[:, s:64:2 * s], tp[:, 0:64:2 * s], tp[:, 2 * s:65:2 * s]

            def clip_low(level):
                mid, own_th, low, _ = tree(level)
                thr_step(v.tensor_tensor, mid, own_th, low, ALU.max)

            def clip_high(level):
                mid, _, _, high = tree(level)
                thr_step(v.tensor_tensor, mid, mid, high, ALU.min)

            clip_low(0)
            par_step(v.tensor_scalar, exi[:, :], k, 127.0, None, ALU.add)
            clip_high(0)
            par_step(v.tensor_scalar, p, r, 1.0 / 5040, None, ALU.mult)
            clip_low(1)
            par_step(v.tensor_scalar, exi[:, :], exi[:, :], 23, None, ALU.logical_shift_left)
            clip_high(1)
            for level, c in ((2, 720), (3, 24), (4, 2)):
                par_step(v.scalar_tensor_tensor, p, p, 1.0 / c, r, ALU.add, ALU.mult)
                clip_low(level)
                par_step(v.scalar_tensor_tensor, p, p, 1.0 / {720: 120, 24: 6, 2: 1}[c], r, ALU.add, ALU.mult)
                clip_high(level)
            e = ex[:, 4, :]
            par_step(v.scalar_tensor_tensor, e, p, 1.0, exi[:, :].bitcast(F32), ALU.add, ALU.mult)
            clip_low(5)
            dt, aa = e[0:H, 0:1], e[0:H, 1:1 + N]
            scale = e[:, 1 + N:]

            xx, w, kk, wr, wc, s1, s2, tt = (pm[:, i, :] for i in (0, 1, 2, 3, 4, 5, 6, 7))
            bb = bim[0:H, :]
            dve.wait_ge(S["par_chain"], n["par_chain"])
            v.tensor_scalar(xx, aa, dt, -1.0, ALU.mult, ALU.mult).then_inc(S["tanh_in"], 1)
            clip_high(5)
            dve.wait_ge(S["in_imag"], 16)
            par_step(v.tensor_scalar, w, bb, dt, None, ALU.mult)
            thr_step(v.tensor_tensor, act_row[:, 0:NTH], tp[:, 1:64], tp[:, 2:65], ALU.is_lt)
            par_step(v.tensor_scalar, kk, w, 0.15915494309189535, ROUND, ALU.mult, ALU.add)
            thr_step(v.tensor_reduce, cnt, act_row[:, 0:NTH], AX_X, ALU.add)
            par_step(v.tensor_scalar, kk, kk, ROUND, None, ALU.subtract)
            dve.wait_ge(S["consts"], 1)
            thr_step(v.tensor_tensor, scr[0:NTH, 0, 0:NTH], act_row[0:NTH, 0:NTH], tri[0:NTH, 0:NTH], ALU.mult)
            par_step(v.scalar_tensor_tensor, wr, kk, -PI2_A, w, ALU.mult, ALU.add)
            thr_step(v.tensor_tensor, scr[0:NTH, 1, 0:NTH], act_row[0:NTH, 0:NTH], ident[0:NTH, 0:NTH], ALU.mult)
            par_step(v.scalar_tensor_tensor, wr, kk, -PI2_B, wr, ALU.mult, ALU.add)
            thr_step(v.tensor_tensor, scr[0:NTH, 2, 0:NTH], tp[0:NTH, 1:64], ident[0:NTH, 0:NTH], ALU.mult)
            par_step(v.scalar_tensor_tensor, wr, kk, -PI2_C, wr, ALU.mult, ALU.add)
            dve.wait_ge(S["par_chain"], n["par_chain"])
            v.tensor_scalar(wc, wr, -3.1415925, 3.1415925, ALU.max, ALU.min).then_inc(S["trig_in"], 1)
            em, q = pm[:, 11, :], pm[:, 13, :]
            dve.wait_ge(S["tanh_done"], 1)
            par_step(v.tensor_scalar, em, tt, -1.0, 1.0, ALU.mult, ALU.add)
            thr_step(v.tensor_tensor, scr[0:NTH, 3, 0:NTH], cb[0:NTH, 1:NCODE], ident[0:NTH, 0:NTH], ALU.mult)
            par_step(v.reciprocal, em, em)
            thr_step(v.tensor_reduce, small[0:NTH, 3:7], scr[0:NTH, :, 0:NTH], AX_X, ALU.add)
            par_step(v.scalar_tensor_tensor, em, tt, 2.0, em, ALU.mult, ALU.mult)
            thr_step(v.tensor_scalar, small[0:NTH, 5:7], small[0:NTH, 5:7], actc[0:NTH, :], None, ALU.mult)
            ep = pp[:, 2, 0:N]
            par_step(v.tensor_scalar, pp[:, 2, 0:N], em, 1.0, None, ALU.add)
            v.tensor_scalar(pp[:, 2, N:], em, 1.0, None, ALU.add)
            v.tensor_scalar(pp[:, 3, 0:N], wr, 0.15915494309189535, None, ALU.mult)
            v.tensor_scalar(pp[:, 3, N:], wr, 0.15915494309189535, None, ALU.mult).then_inc(S["params"], 1)

            dve.wait_ge(S["trig_done"], 1)
            thr_step(v.tensor_scalar, slot_rhs[0:NTH, 0, :], ramp1[0:NTH, :], rank[0:NTH, :], tcol[0:NTH, :], ALU.is_equal, ALU.mult)
            par_step(v.tensor_tensor, q, s2, s2, ALU.mult)
            v.tensor_copy(n_int[:, :], cnt)
            thr_step(v.tensor_scalar, slot_rhs[0:NTH, 1, :], ramp1[0:NTH, :], rank[0:NTH, :], ccol[0:NTH, :], ALU.is_equal, ALU.mult)
            v.tensor_scalar(over[:, :], ramp1[:, :], cnt, BIG, ALU.is_gt, ALU.mult).then_inc(S["slot_ready"], 1)
            par_step(v.scalar_tensor_tensor, q, q, 2.0, ep, ALU.mult, ALU.mult)
            v.reciprocal(inv_scale[:, :], scale).then_inc(S["scale_ready"], 1)
            dve.wait_ge(S["scale_ready"], 1)

            dve.wait_ge(S["params_T"], 1)
            v.tensor_copy(par[:, 2:4, :], psA[:, 0:2 * H].rearrange("p (k h) -> p k h", h=H)).then_inc(S["par_ready"], 1)
            tau, tw = par[:, 3, :], tau32[:, 0, :]
            dve.wait_ge(S["par_ready"], 1)
            par_step(v.tensor_scalar, tau32[:, 1, :], tau, 32.0, ROUND, ALU.mult, ALU.add)
            v.tensor_tensor(tV[:, :, :], tau.unsqueeze(2).to_broadcast([P, H, RS]),
                            ramp[:, 0:RS].unsqueeze(1).to_broadcast([P, H, RS]), ALU.mult).then_inc(S["thr_chain"], 1)
            n["thr_chain"] += 1
            par_step(v.tensor_scalar, tau32[:, 1, :], tau32[:, 1, :], ROUND, None, ALU.subtract)
            thr_step(v.tensor_scalar, fV[:, :, :], tV[:, :, :], phase[:, 0:1], ROUND, ALU.add, ALU.add)
            par_step(v.scalar_tensor_tensor, tw, tau, 32.0, tau32[:, 1, :], ALU.mult, ALU.subtract)
            par_step(v.tensor_tensor, tU[:, :, :], tw.unsqueeze(2).to_broadcast([P, H, AS]),
                     ramp[:, 0:AS].unsqueeze(1).to_broadcast([P, H, AS]), ALU.mult)
            par_step(v.tensor_scalar, fU[:, 0, :, :], tU[:, :, :], 0.25, ROUND, ALU.add, ALU.add)
            v.tensor_scalar(fU[:, 1, :, :], tU[:, :, :], ROUND, None, ALU.add).then_inc(S["par_chain"], 1)
            dve.wait_ge(S["par_chain"], n["par_chain"])
            v.scalar_tensor_tensor(fU[:, 0, :, :], fU[:, 0, :, :], ROUND, tU[:, :, :], ALU.subtract, ALU.subtract).then_inc(S["sinU_in"], 1)
            n["par_chain"] += 1
            dve.wait_ge(S["par_chain"], n["par_chain"])
            v.scalar_tensor_tensor(fU[:, 1, :, :], fU[:, 1, :, :], ROUND, tU[:, :, :], ALU.subtract, ALU.subtract).then_inc(S["sinU_in"], 1)
            dve.wait_ge(S["thr_chain"], n["thr_chain"])
            v.scalar_tensor_tensor(fV[:, :, :], fV[:, :, :], ROUND, tV[:, :, :], ALU.subtract, ALU.subtract).then_inc(S["sinV_in"], 1)

            dve.wait_ge(S["trig_done"], 2)
            a2, b2, inv = (pm[:, i, :] for i in (8, 9, 10))
            v.tensor_tensor(pm[:, 14, :], em, q, ALU.subtract)
            v.tensor_tensor(a2, aa, aa, ALU.mult)
            v.tensor_tensor(b2, bb, bb, ALU.mult)
            par_step(v.tensor_tensor, pm[:, 15, :], ep, s1, ALU.mult)
            par_step(v.tensor_tensor, a2, a2, b2, ALU.add)
            E = pm[:, 14:16, :]
            aE, bE, G, c0G, c1G = pm[:, 16:18, :], pm[:, 18:20, :], pm[:, 20:22, :], pm[:, 22:24, :], pm[:, 0:2, :]
            a_b = aa.unsqueeze(1).to_broadcast([H, 2, N])
            b_b = bb.unsqueeze(1).to_broadcast([H, 2, N])
            v.tensor_tensor(aE, E, a_b, ALU.mult)
            par_step(v.tensor_tensor, bE, E, b_b, ALU.mult)
            par_step(v.reciprocal, inv, a2)
            v.tensor_tensor(pm[:, 20, :], pm[:, 19, :], pm[:, 16, :], ALU.subtract)
            par_step(v.tensor_tensor, pm[:, 21, :], pm[:, 18, :], pm[:, 17, :], ALU.add)
            par_step(v.scalar_tensor_tensor, G, G, 2.0, inv.unsqueeze(1).to_broadcast([H, 2, N]), ALU.mult, ALU.mult)
            dve.wait_ge(S["in_c"], 16)
            c0 = cin[0:H, :, 0].unsqueeze(1).to_broadcast([H, 2, N])
            c1 = cin[0:H, :, 1].unsqueeze(1).to_broadcast([H, 2, N])
            dve.wait_ge(S["par_chain"], n["par_chain"])
            v.tensor_tensor(c0G, G, c0, ALU.mult)
            par_step(v.tensor_tensor, c1G, G, c1, ALU.mult)
            dve.wait_ge(S["par_chain"], n["par_chain"])
            v.tensor_tensor(pp[:, 0, N:], pm[:, 23, :], pm[:, 0, :], ALU.subtract)
            v.tensor_tensor(pp[:, 1, 0:N], pm[:, 23, :], pm[:, 0, :], ALU.subtract)
            par_step(v.tensor_tensor, pp[:, 0, 0:N], pm[:, 22, :], pm[:, 1, :], ALU.add)
            dve.wait_ge(S["par_chain"], n["par_chain"])
            v.tensor_scalar(pp[:, 1, N:], pp[:, 0, 0:N], -1.0, None, ALU.mult).then_inc(S["params"], 1)

            dve.wait_ge(S["params_T"], 2)
            par_step(v.tensor_copy, par[:, 0:2, :], psC[3][:, 0:2 * H].rearrange("p (k h) -> p k h", h=H))
            dve.wait_ge(S["sin_done"], 2)
            dve.wait_ge(S["mags"], 1)
            for k in range(2):
                hs = slice(k * H // 2, (k + 1) * H // 2)
                al = par[:, 0, hs].unsqueeze(2).to_broadcast([P, H // 2, AS])
                be = par[:, 1, hs].unsqueeze(2).to_broadcast([P, H // 2, AS])
                dve.wait_ge(S["par_chain"], n["par_chain"])
                v.tensor_tensor(sU[:, 0, hs, :], sU[:, 0, hs, :], al, ALU.mult)
                par_step(v.tensor_tensor, sU[:, 1, hs, :], sU[:, 1, hs, :], be, ALU.mult)
                par_step(v.tensor_tensor, sU[:, 0, hs, :], sU[:, 0, hs, :], sU[:, 1, hs, :], ALU.add)
                dve.wait_ge(S["par_chain"], n["par_chain"])
                v.tensor_tensor(tU[:, hs, ::-1], sU[:, 0, hs, :], magU[:, hs, :], ALU.mult).then_inc(S["kfac"], 1)

            v.tensor_reduce(own[:, :], ident[:, :].rearrange("p (h b) -> p b h", b=GB), AX_X, ALU.add).then_inc(S["own_ready"], 1)
            dve.wait_ge(S["masks"], 1)
            dve.wait_ge(S["own_ready"], 1)
            par_step(v.reciprocal, linv[:, :], lenf[:, 1, :])
            par_step(v.tensor_tensor, lown[:, :, :], linv[:, :].rearrange("p (g b) -> p g b", b=GB),
                     own[:, :].unsqueeze(1).to_broadcast([P, NG, GB]), ALU.mult)
            par_step(v.tensor_reduce, linv_own[:, :], lown[:, :, :], AX_X, ALU.add)

            m = [0]

            def link(ins):
                m[0] += 1
                ins.then_inc(S["dve_chain"], 1)
                dve.wait_ge(S["dve_chain"], m[0])

            v.tensor_copy(quant[:, :, :], cb[:, 0:1].unsqueeze(2).to_broadcast([P, 4, L]))
            dve.wait_ge(S["slot_done"], 1)
            v.tensor_copy(slots[:, :, :], psC[2][:, 0:128].rearrange("p (k j) -> p k j", k=2)).then_inc(S["slots_sb"], 1)
            dve.wait_ge(S["slots_sb"], 1)
            link(v.tensor_tensor(slots[:, 0, :], slots[:, 0, :], over[:, :], ALU.add))
            for t in range(4):
                dve.wait_ge(S["raw_ready"], t + 1)
                link(v.tensor_tensor(nrm[:, t, :].rearrange("p (g k) -> p g k", k=P), w_in[:, t, :].rearrange("p (g k) -> p g k", k=P),
                                     inv_scale[:, 4 * t:4 * t + 4].unsqueeze(2).to_broadcast([P, 4, P]), ALU.mult))
            for j in range(FAST_SLOTS):
                link(v.tensor_scalar(msk[:, :, :], nrm[:, :, :], slots[:, 0, j:j + 1], None, ALU.is_gt))
                link(v.copy_predicated(quant[:, :, :], msk[:, :, :],
                                       slots[:, 1, j:j + 1].unsqueeze(2).to_broadcast([P, 4, L])))
            n_slots = dve.value_load(n_int[0:1, 0:1], min_val=1, max_val=NTH)
            with dve.If(n_slots > FAST_SLOTS):
                with dve.Fori(FAST_SLOTS, NTH) as j:
                    v.tensor_copy(cur[:, 0:2], slots[:, :, bass.ds(j, 1)].rearrange("p a b -> p (a b)")).then_inc(S["dve_loop"], 1)
                    dve.wait_ge(S["dve_loop"], j * 3 - (3 * FAST_SLOTS - 1))
                    v.tensor_scalar(msk[:, :, :], nrm[:, :, :], cur[:, 0:1], None, ALU.is_gt).then_inc(S["dve_loop"], 1)
                    dve.wait_ge(S["dve_loop"], j * 3 - (3 * FAST_SLOTS - 2))
                    v.tensor_copy(cur[:, 2:3], cur[:, 0:1])
                    v.copy_predicated(quant[:, :, :], msk[:, :, :],
                                      cur[:, 1:2].unsqueeze(2).to_broadcast([P, 4, L])).then_inc(S["dve_loop"], 1)
                    dve.wait_ge(S["dve_loop"], j * 3 - (3 * FAST_SLOTS - 3))

            def weff(t):
                q, m = quant[:, t, :], nrm[:, t, :]
                link(v.tensor_tensor(q, q, m, ALU.subtract))
                link(v.tensor_tensor(q, q, m, ALU.add))
                q3 = q.rearrange("p (g k) -> p g k", k=P)
                link(v.tensor_tensor(q3, q3, scale[:, 4 * t:4 * t + 4].unsqueeze(2).to_broadcast([P, 4, P]), ALU.mult))
                link(v.tensor_tensor(q, q, dlt[:, t, :], ALU.add))
                qd = q[:, t * P:(t + 1) * P]
                v.tensor_tensor(qd, qd, ident[:, :], ALU.add).then_inc(S["weff"], 1)

            def add_halves(i):
                dve.wait_ge(S["mhalf_ready"], i + 1)
                h2 = mhalf[:, i % 4, :].rearrange("p (k g n) -> p k g n", k=2, g=NG)
                dst = msum[:, :, 2 * i * GB:(2 * i + 2) * GB]
                v.tensor_tensor(dst, h2[:, 0], h2[:, 1], ALU.add).then_inc(S["mhalf_used"], 1)

            def lower(i):
                dve.wait_ge(S["hi_ready"], i + 1)
                dve.wait_ge(S["masked"], i + 1)
                pair = slice(2 * i, 2 * i + 2)
                v.tensor_tensor(x_lo[:, :, :, pair, :].rearrange("p c g h b -> p (c g) h b"),
                                xT[:, :, :, pair, :].rearrange("p c g h b -> p (c g) h b"),
                                x_hi[:, :, :, pair, :].bitcast(F32).rearrange("p c g h b -> p (c g) h b"),
                                ALU.subtract).then_inc(S["lo_ready"], 1)

            def mt_lower(c):
                dve.wait_ge(S["mt_hi_sb"], c + 1)
                v.tensor_tensor(mt_lo[:, c, :], psX[c % 2][:, :], mt_hi[:, c, :].bitcast(F32), ALU.subtract).then_inc(S["mt_lo_sb"], 1)

            dve.wait_ge(S["xt_sb"], NG)
            for i in range(NPAIR):
                dve.wait_ge(S["conv_done"], i + 1)
                dst = xT[:, :, :, 2 * i:2 * i + 2, :].rearrange("p c g h b -> p h (c g) b")
                kp = keep[:, :, :].rearrange("p c (g b) -> p (c g) b", b=GB).unsqueeze(1).to_broadcast([P, 2, NC * NG, GB])
                v.copy_predicated(dst, kp, psC[i % 4][:, :].rearrange("p (h n b) -> p h n b", h=2, b=GB)
                                  ).then_inc(S["conv_used"], 1)
                if i >= 3:
                    add_halves(i - 3)
                if i in (1, 3, 5, 7):
                    weff(i // 2)
                if i >= 2:
                    lower(i - 2)
                if 11 <= i < 15:
                    dve.wait_ge(S["g_hi_ready"], i - 10)
                    q = slice(4 * (i - 11), 4 * (i - 10))
                    v.tensor_tensor(g_lo[:, q, :], gmat[:, q, :], g_hi[:, q, :].bitcast(F32), ALU.subtract).then_inc(S["g_lo_ready"], 1)
                if i >= 13:
                    mt_lower(i - 13)
            lower(NPAIR - 2)
            mt_lower(3)
            lower(NPAIR - 1)
            for i in range(NPAIR - 3, NPAIR):
                add_halves(i)
            dve.wait_ge(S["ymean"], 1)
            v.tensor_tensor(gmean[:, :], psA[:, 0:NG], linv_own[:, :], ALU.mult).then_inc(S["gmean_ready"], 1)
            dve.wait_ge(S["gate_th"], 1)
            v.tensor_scalar(gate[:, :], gth[:, :], 0.5, 1.5, ALU.mult, ALU.add).then_inc(S["gated"], 1)
            dve.wait_ge(S["gated"], 1)

            def y_lower(g):
                dve.wait_ge(S["y_hi_sb"], g + 1)
                v.scalar_tensor_tensor(y_lo[:, g % 4, :], psC[g % 4][:, :], gate[:, g:g + 1], y_hi[:, g % 4, :].bitcast(F32),
                                       ALU.mult, ALU.subtract).then_inc(S["y_sb"], 1)

            def out_rows(g):
                dve.wait_ge(S["o_done"], g + 1)
                if g >= 4:
                    dve.wait_ge(stored[g % 4], 16 * (g // 4))
                v.tensor_copy(osb[:, g % 4, :], psX[g % 2][:, :]).then_inc(S["o_sb"], 1)

            for g in range(NG):
                y_lower(g)
                if g >= MIX_LAG:
                    out_rows(g - MIX_LAG)
            for g in range(NG - MIX_LAG, NG):
                out_rows(g)

        @block.tensor
        def _(pe):
            m = nc.tensor
            pe.wait_ge(S["consts"], 1)
            pe.wait_ge(S["in_lb"], 16)
            for t in range(4):
                last = m.transpose(psB[0:R, t * P:(t + 1) * P], lb[:, t, :], ident[:, :])
            last.then_inc(S["lbT_done"], 1)
            pe.wait_ge(S["in_la"], 16)
            pe.wait_ge(S["lbT_sb"], 1)
            def delta(t):
                m.matmul(psC[t][:, :], lbT[:, t * P:(t + 1) * P], la[:, :], start=True, stop=True).then_inc(S["delta_done"], 1)

            def x_transposes(g):
                pe.wait_ge(in_x[g], 16)
                if g >= 2:
                    pe.wait_ge(S["xt_sb"], g - 1)
                else:
                    pe.wait_ge(S["sel_sb"], g + 1)
                for c in range(NC):
                    last = m.transpose(psX[g % 2][:, c * P:(c + 1) * P], xrows[:, g, c * P:(c + 1) * P], ident[:, :])
                last.then_inc(S["xt_done"], 1)

            def param_transposes(k0, bank, n):
                pe.wait_ge(S["params"], n)
                for k in range(k0, k0 + 2):
                    last = m.transpose(bank[:, (k - k0) * H:(k - k0 + 1) * H], pp[:, k, :], ident[0:H, 0:H])
                last.then_inc(S["params_T"], 1)

            def d_at_zero():
                pe.wait_ge(S["drow_ready"], 1)
                pe.wait_ge(S["par_ready"], 1)
                for k, bank in ((0, psA), (1, psB)):
                    m.matmul(bank[0:AS, :], last_a[0:1, :], drow[:, k * H // 2:(k + 1) * H // 2, :].rearrange("p h r -> p (h r)"),
                             start=True, stop=False, skip_group_check=True)

            delta(0)
            delta(1)
            pe.wait_ge(S["sel_oh"], 1)
            pe.wait_ge(S["in_wall"], 16)
            for i in range(2):
                m.matmul(psX[i][0:B, :], onehot[:, :], wall[:, i * 512:(i + 1) * 512], start=True, stop=True).then_inc(S["sel_done"], 1)
            param_transposes(2, psA, 1)
            delta(2)
            delta(3)
            for g in range(X_BEFORE_K):
                x_transposes(g)
                if g == 1:
                    d_at_zero()
                if g == T2_AT:
                    pe.wait_ge(S["delta_sb"], 4)
                    param_transposes(0, psC[3], 2)
            for k, bank in ((0, psA), (1, psB)):
                pe.wait_ge(S["kfac_v"], k + 1)
                pe.wait_ge(S["kfac"], k + 1)
                for j in range(H // 2):
                    h = k * H // 2 + j
                    last = m.matmul(bank[0:AS, j * RS:(j + 1) * RS], tU[:, h, :], sV[:, h, :],
                                    start=False, stop=True, skip_group_check=True)
                last.then_inc(S["k_done"], 1)
            pe.wait_ge(S["slot_ready"], 1)
            m.matmul(psC[2][:, 0:128], ones[0:NTH, :], slot_rhs[0:NTH, :, :].rearrange("p k j -> p (k j)"),
                     start=True, stop=True).then_inc(S["slot_done"], 1)
            for g in range(X_BEFORE_K, NG):
                x_transposes(g)
            def weff_transposes(c):
                if c == 0:
                    pe.wait_ge(S["weff"], 4)
                if c >= 2:
                    pe.wait_ge(S["mt_lo_sb"], c - 1)
                for t in range(4):
                    last = m.transpose(psX[c % 2][:, t * P:(t + 1) * P], quant[:, t, c * P:(c + 1) * P], ident[:, :])
                last.then_inc(S["wT_done"], 1)

            for i in range(NPAIR):
                if i == 2:
                    pe.wait_ge(S["slots_sb"], 1)
                pe.wait_ge(S["turned"], i + 1)
                if i >= 4:
                    pe.wait_ge(S["conv_used"], i - 3)
                for j in range(2):
                    h = 2 * i + j
                    xh = xT[:, :, :, h, :].rearrange("p c g b -> p (c g) b")
                    for d in range(NC):
                        n = (NC - d) * B
                        o = j * NC * B + d * B
                        last = m.matmul(psC[i % 4][:, o:o + n], toep[:, i % NSLOT, j, d * P:(d + 1) * P], xh[:, 0:n // GB, :],
                                        start=(d == 0), stop=(d == NC - 1), skip_group_check=True)
                last.then_inc(S["conv_done"], 1)
                if i >= 12:
                    weff_transposes(i - 12)

            def rows(part, g, c):
                return part[:, c, g, :, :].rearrange("p h b -> p (h b)")

            def times_m(g):
                if g >= 4:
                    pe.wait_ge(S["y_sb"], g - 3)
                bank = psC[g % 4]
                for c in range(NC):
                    if g == 0:
                        pe.wait_ge(S["mt_hi_sb"], c + 1)
                    m.matmul(bank[:, :], rows(x_hi, g, c), mt_hi[:, c, :], start=(c == 0), stop=False)
                    if g == 0:
                        pe.wait_ge(S["mt_lo_sb"], c + 1)
                    m.matmul(bank[:, :], rows(x_hi, g, c), mt_lo[:, c, :], start=False, stop=False)
                if g == 0:
                    pe.wait_ge(S["lo_ready"], NPAIR)
                for c in range(NC):
                    last = m.matmul(bank[:, :], rows(x_lo, g, c), mt_hi[:, c, :], start=False, stop=(c == NC - 1))
                last.then_inc(S["y_done"], 1)

            def mix(g):
                pe.wait_ge(S["y_sb"], g + 1)
                if g >= 2:
                    pe.wait_ge(S["o_sb"], g - 1)
                bank = psX[g % 2]
                m.matmul(bank[:, :], g_hi[:, g, :], y_hi[:, g % 4, :], start=True, stop=False)
                m.matmul(bank[:, :], g_hi[:, g, :], y_lo[:, g % 4, :], start=False, stop=False)
                m.matmul(bank[:, :], g_lo[:, g, :], y_hi[:, g % 4, :], start=False, stop=True).then_inc(S["o_done"], 1)

            pe.wait_ge(S["hi_ready"], NPAIR)
            for g in range(NG):
                if g == 1:
                    pe.wait_ge(S["mhalf_used"], NPAIR)
                    for k in range(NG):
                        last = m.matmul(psA[:, k:k + 1], msum[:, k, :], ones[:, 0:1], start=True, stop=True, skip_group_check=True)
                    last.then_inc(S["ymean"], 1)
                times_m(g)
                if g == 1:
                    pe.wait_ge(S["gmean_ready"], 1)
                    pe.wait_ge(S["cmat_ready"], 1)
                    m.matmul(psB[:, 0:NG], cmat[:, :], gmean[:, :], start=True, stop=True).then_inc(S["chan"], 1)
                if g == MIX_LAG:
                    pe.wait_ge(S["g_lo_ready"], 4)
                if g >= MIX_LAG:
                    mix(g - MIX_LAG)
            for g in range(NG - MIX_LAG, NG):
                mix(g)


_INS = ['x', 'itok_B_78_3631', 'itok_B_9_3973', 'condB_codebook', 'itok_B_0_15', 'L0_cond_log_dt', 'L0_cond_C',
        'L0_cond_log_A_real', 'L0_cond_A_imag', 'L0_cond_D', 'L1_cond_conv_w', 'L2_cond_weight', 'L2_cond_scale_log',
        'L2_cond_lora_A', 'L2_cond_lora_B', 'L3_cond_weights']
_OUTS = [((64, 32, 512), 'float32')]


def kernel(**inputs):
    import numpy as _np
    import concourse.bacc as _bacc
    from concourse import mybir as _mybir
    from concourse.bass_utils import run_bass_kernel_spmd as _run

    nc = _bacc.Bacc("TRN2", target_bir_lowering=False, num_devices=1)
    arrays, args = {}, []
    for name in _INS:
        a = _np.ascontiguousarray(inputs[name])
        arrays[f"in_{name}_dram"] = a
        args.append(nc.dram_tensor(f"in_{name}_dram", a.shape, _mybir.dt.from_np(a.dtype), kind="ExternalInput").ap())
    for i, (shape, dtype) in enumerate(_OUTS):
        dt = _mybir.dt.from_np(_np.dtype(dtype))
        args.append(nc.dram_tensor(f"out_{i}_dram", shape, dt, kind="ExternalOutput").ap())
    cond_resid_kernel(nc, *args)
    r = _run(nc, [arrays], core_ids=[0])
    got = tuple(r.results[0][f"out_{i}_dram"] for i in range(len(_OUTS)))
    return got[0]
```

```python
from contextlib import ExitStack

import concourse.bass as bass
from concourse import mybir

ALU = mybir.AluOpType
ACT = mybir.ActivationFunctionType
F32 = mybir.dt.float32
I32 = mybir.dt.int32
F32R = mybir.dt.float32r
AX_X = mybir.AxisListType.X

P = 128
TWO_PI = 6.2831850
ROUND = 12582912.0
BIG = 3.0e38
LN2_HI, LN2_LO = 0.693359375, -2.12194440e-4
PI2_A, PI2_B, PI2_C = 6.28125, 1.9350051879882812e-3, 3.0199159819e-7
NB = 4
X_BEFORE_K, SIN_AT = 4, 0
X_ON_DVE = (5, 7, 9, 12, 15)
MERGES = (1, 2)
EARLY_TAPS = 2
POOL_LOWER = (0,)
LATE_LOWER = 8
CATCH_UP = 12
UPPER_LAG = 4
FAST_SLOTS = 3


def cond_resid_kernel(nc, x, len_conv, len_gate, codebook, cond, log_dt, C, log_A_real, A_imag, D, conv_w,
                      weight, scale_log, lora_A, lora_B, cond_W, out):
    B, H, L = x.shape
    N = A_imag.shape[1]
    NC = L // P
    GB = P // H
    NG = B // GB
    NPAIR = H // 2
    NCODE = codebook.shape[0]
    NTH = NCODE - 1
    R = lora_A.shape[0]
    NK = cond_W.shape[0]
    TAPS = conv_w.shape[2]
    AS, RS = L // 32, 32
    NSLOT = 3
    PAD = L + P

    with ExitStack() as ctx:
        def sb(name, shape, dt=F32):
            return ctx.enter_context(nc.sbuf_tensor(name, shape, dt))

        def spent(name, shape, dt=F32):
            with nc.sbuf_tensor(name, shape, dt) as buffer:
                return buffer

        def sem(name):
            return ctx.enter_context(nc.semaphore(name))

        psX = [ctx.enter_context(nc.psum_tensor(f"psX{i}", [P, 512], F32)) for i in range(2)]
        psA = ctx.enter_context(nc.psum_tensor("psA", [P, 512], F32))
        psB = ctx.enter_context(nc.psum_tensor("psB", [P, 512], F32))
        psC = [ctx.enter_context(nc.psum_tensor(f"psC{i}", [P, 512], F32)) for i in range(4)]

        kpad = nc.dram_tensor("kpad", [H, PAD], F32, kind="Internal")
        wsel_dram = nc.dram_tensor("wsel_dram", [B, H * H], F32, kind="Internal")

        xrows = spent("xrows", [P, NG, L])
        x_hi = sb("x_hi", [P, NC, NG, H, GB], F32R)
        w_in = sb("w_in", [P, 4, L])
        la = sb("la", [R, L])
        lb = sb("lb", [P, 4, R])
        lns = sb("lns", [P, 1 + N + 16])
        bim = sb("bim", [P, N])
        cin = sb("cin", [P, N, 2])
        drow = sb("drow", [1, H, RS])
        dcol = sb("dcol", [1, H])
        last_a = sb("last_a", [P, AS])
        cb = sb("cb", [P, NCODE])
        cwt = sb("cwt", [P, TAPS])
        leni = sb("leni", [P, 2, B], I32)
        condi = sb("condi", [NK, B], I32)
        wall = sb("wall", [NK, H * H])

        diff = sb("diff", [P, P])
        ident = sb("ident", [P, P])
        tri = sb("tri", [P, P])
        own = sb("own", [P, GB])
        pcol = sb("pcol", [P, 1])
        ramp = sb("ramp", [P, 64])
        ramp1 = sb("ramp1", [P, 64])
        phase = sb("phase", [P, 1])
        phase_rad = sb("phase_rad", [P, 1])
        quarter_rad = sb("quarter_rad", [P, 1])
        ones = sb("ones", [P, P])
        zpad = sb("zpad", [H, P])

        ex = sb("ex", [P, 6, 1 + N + 16])
        exi = sb("exi", [P, 1 + N + 16], I32)
        pm = sb("pm", [H, 24, N])
        pp = sb("pp", [H, 4, 2 * N])
        par = sb("par", [P, 4, H])
        sq = sb("sq", [P, 8, H])
        magV = sb("magV", [P, H, RS])
        magU = sb("magU", [P, H, AS])
        tau32 = sb("tau32", [P, 2, H])
        tV = sb("tV", [P, H, RS])
        tU = sb("tU", [P, H, AS])
        fV = sb("fV", [P, H, RS])
        fU = sb("fU", [P, 2, H, AS])
        sV, sU = fV, fU
        ksb = sb("ksb", [AS, H, RS])

        th = sb("th", [P, 64])
        tp = sb("tp", [P, 65])
        act_row = sb("act_row", [P, 64])
        scr = sb("scr", [P, 4, 64])
        small = sb("small", [P, 16])
        slot_rhs = sb("slot_rhs", [64, 2, 64])
        slots = sb("slots", [P, 2, 64])
        over = sb("over", [P, 64])
        n_int = sb("n_int", [P, 1], I32)
        cur = sb("cur", [P, 3])
        inv_scale = sb("inv_scale", [P, 16])
        lbT = sb("lbT", [R, L])
        dlt = spent("dlt", [P, 4, L])
        g_hi = sb("g_hi", [P, NG, P], F32R)
        nrm = spent("nrm", [P, 4, L])
        mt_lo = sb("mt_lo", [P, NC, L], F32R)
        msk = spent("msk", [P, 4, L], I32)
        mt_hi = sb("mt_hi", [P, NC, L], F32R)
        quant = sb("quant", [P, 4, L])

        lenf = sb("lenf", [P, 2, B])
        keep = sb("keep", [P, NC, B], I32)
        mask2 = sb("mask2", [P, NC, B])
        linv = sb("linv", [P, B])
        xT = spent("xT", [P, NC, NG, H, GB])
        x_lo = sb("x_lo", [P, NC, NG, H, GB], F32R)
        with nc.sbuf_tensor("toep", [P, NSLOT, 2, L], F32) as toep:
            hank = spent("hank", [P, NSLOT, 2, L])
        y_hi = sb("y_hi", [P, 4, L], F32R)
        y_lo = sb("y_lo", [P, 4, L], F32R)
        osb = sb("osb", [P, 4, L])
        cmat = sb("cmat", [P, P])
        ctmp = sb("ctmp", [P, P])
        lown = sb("lown", [P, NG, GB])
        linv_own = sb("linv_own", [P, NG])
        mtmp = fU[:, 0, :, :].rearrange("p h a -> p (h a)")
        mhalf = tV[:, :, :].rearrange("p h r -> p (h r)").rearrange("p (s n) -> p s n", s=4)
        msum = w_in[:, :, :].rearrange("p t i -> p (t i)").rearrange("p (g n) -> p g n", g=NG)
        out_slots = [osb[:, i, :] for i in range(4)] + [quant[:, i, :] for i in range(4)]
        gsum = sb("gsum", [P, NG])
        gmean = sb("gmean", [P, NG])
        gth = sb("gth", [P, NG])
        gate = sb("gate", [P, NG])
        condf = sb("condf", [NK, B])
        onehot = sb("onehot", [NK, B])
        wsel = sb("wsel", [B, H * H])
        wrows = sb("wrows", [P, NG, H])
        gmat = spent("gmat", [P, NG, P])
        g_lo = sb("g_lo", [P, NG, P], F32R)

        S = {n: sem(n) for n in (
            "in_lns in_imag in_c in_d in_cb in_cw in_len in_cond in_w in_la in_lb in_wall "
            "consts pool_chain par_chain thr_chain dve_chain dve_loop "
            "drow_ready tV_ready pad_written k_written tanh_in tanh_done trig_in trig_done params params_T par_ready mags "
            "sinV_in sinU_in sin_done kfac kfac_v k_done ksb_ready scale_ready raw_ready "
            "lbT_done lbT_sb delta_done delta_sb sel_oh sel_done sel_sb sel_written sel_loaded "
            "xt_done slot_ready slot_done turned_first turned conv_done conv_used mhalf_ready mhalf_used "
            "weff wT_done mt_hi_sb mt_lo_sb ste_ready scaled masks own_ready slots_sb masked gmat_ready g_hi_ready g_lo_ready hi_ready lo_ready ymean gsum_ready gmean_ready chan gate_th gated y_hi_sb o_sb_act "
            "y_done y_sb o_done o_sb").split()}
        k_written = [sem(f"k_written{i}") for i in range(2)]
        xt_sb = [sem(f"xt_sb{i}") for i in range(4)]
        in_x = [sem(f"in_x{i}") for i in range(NG)]
        in_hank = [sem(f"in_hank{i}") for i in range(NSLOT)]
        stored = [sem(f"stored{i}") for i in range(8)]

        x_rows = x.rearrange("(g b) h l -> g h b l", b=GB)
        o_rows = out.rearrange("(g b) h l -> g h b l", b=GB)

        x_banks = (psX[0], psX[1], psC[0], psC[1])
        wT_banks = (psX[0], psX[1], psA, psB)
        mean_banks = (psX[0], psX[1], psA, psB)
        o_banks = (psX[0], psX[1], psA, psB)

        ALL, HALVES = slice(0, L), (slice(0, L // 2), slice(L // 2, L))

        def mixed_before(g):
            return max(0, min(g - NB + 1 + max(0, g - CATCH_UP), g - 1))

        def hankel_rows(i):
            return bass.AP(kpad, 2 * i * PAD, [[1, P], [PAD, 2], [1, L]])

        block = ctx.enter_context(nc.Block())

        @block.sync
        def _(sp):
            sp.dma_start(lns[:, 1:1 + N], bass.AP(log_A_real.tensor, 0, [[0, GB], [N, H], [1, N]])).then_inc(S["in_lns"], 16)
            sp.dma_start(lns[:, 1 + N:].rearrange("p (t g) -> p t g", t=4),
                         scale_log.rearrange("(t p) g k -> p t (g k)", p=P)).then_inc(S["in_lns"], 16)
            sp.dma_start(bim[:, :], bass.AP(A_imag.tensor, 0, [[0, GB], [N, H], [1, N]])).then_inc(S["in_imag"], 16)
            sp.dma_start(cin[:, :, :], bass.AP(C.tensor, 0, [[0, GB], [2 * N, H], [2, N], [1, 2]])).then_inc(S["in_c"], 16)
            sp.dma_start(condi[:, :], bass.AP(cond.tensor, 0, [[0, NK], [1, B]])).then_inc(S["in_cond"], 16)
            sp.dma_start(wall[:, :], cond_W.rearrange("k c d -> k (c d)")).then_inc(S["in_wall"], 16)
            sp.dma_start(leni[:, 0, :], bass.AP(len_conv.tensor, 0, [[0, P], [1, B]])).then_inc(S["in_len"], 16)
            sp.dma_start(leni[:, 1, :], bass.AP(len_gate.tensor, 0, [[0, P], [1, B]])).then_inc(S["in_len"], 16)
            sp.dma_start(dcol[:, :], D.rearrange("(o h) -> o h", o=1)).then_inc(S["in_d"], 16)
            for g in range(NG):
                sp.dma_start(xrows[:, g, :], x_rows[g]).then_inc(in_x[g], 16)
                if g == 3:
                    sp.dma_start(w_in[:, :, :], weight.rearrange("(t p) i -> p t i", p=P)).then_inc(S["in_w"], 16)
            sp.wait_ge(S["consts"], 1)
            sp.dma_start(kpad[:, L:PAD], zpad[:, :]).then_inc(S["pad_written"], 16)
            sp.wait_ge(S["sel_sb"], 2)
            sp.dma_start(wsel_dram[:, :], wsel[:, :]).then_inc(S["sel_written"], 16)
            sp.wait_ge(S["sel_written"], 16)
            for b in range(GB):
                sp.dma_start(wrows[b:P:GB, :, :], bass.AP(wsel_dram, b * H * H, [[H, H], [GB * H * H, NG], [1, H]])
                             ).then_inc(S["sel_loaded"], 16)
            sp.wait_ge(S["pad_written"], 16)
            for i in range(NPAIR):
                if i % (NPAIR // 2) == 0:
                    sp.wait_ge(k_written[i // (NPAIR // 2)], 16)
                if i >= NSLOT:
                    sp.wait_ge(S["turned"], i - NSLOT + 1)
                sp.dma_start(hank[:, i % NSLOT, :, :], hankel_rows(i)).then_inc(in_hank[i % NSLOT], 16)
            for g in range(NG):
                if g < NG - 2:
                    sp.wait_ge(S["o_sb"], g + 1)
                elif g == NG - 2:
                    sp.wait_ge(S["o_sb_act"], 1)
                else:
                    sp.wait_ge(S["o_sb_act"], 2)
                    sp.wait_ge(S["o_sb"], NG - 1)
                sp.dma_start(o_rows[g], out_slots[g % 8]).then_inc(stored[g % 8], 16)
            for i in range(8):
                sp.wait_ge(stored[i], 16 * (NG // 8))

        @block.gpsimd
        def _(pool):
            n = [0]

            def link(ins):
                n[0] += 1
                ins.then_inc(S["pool_chain"], 1)
                pool.wait_ge(S["pool_chain"], n[0])

            g = nc.gpsimd
            g.iota(diff[:, :], [[1, P]], base=0, channel_multiplier=-1, allow_small_or_imprecise_dtypes=True)
            g.iota(pcol[:, :], [[0, 1]], base=0, channel_multiplier=1, allow_small_or_imprecise_dtypes=True)
            g.iota(ramp[:, :], [[1, 64]], base=0, channel_multiplier=0, allow_small_or_imprecise_dtypes=True)
            link(g.iota(ramp1[:, :], [[1, 64]], base=1, channel_multiplier=0, allow_small_or_imprecise_dtypes=True))
            g.tensor_scalar(tri[:, :], diff[:, :], 0.0, None, ALU.is_le)
            g.tensor_scalar(ident[:, :], diff[:, :], 0.0, None, ALU.is_equal)
            g.memset(zpad[:, :], 0.0)
            g.memset(ones[:, :], 1.0)
            g.memset(quarter_rad[:, :], 0.25 * TWO_PI)
            g.tensor_scalar(phase[:, :], pcol[:, :], float(N), 0.25, ALU.is_lt, ALU.mult)
            g.tensor_scalar(phase_rad[:, :], pcol[:, :], float(N), 0.25 * TWO_PI, ALU.is_lt, ALU.mult)
            g.tensor_scalar(last_a[:, :], ramp[:, 0:AS], float(AS - 1), None, ALU.is_equal).then_inc(S["consts"], 1)
            link(g.memset(drow[:, :, :], 0.0))
            pool.wait_ge(S["in_d"], 16)
            g.tensor_scalar(drow[:, :, 0], dcol[:, :], 1.0, None, ALU.add).then_inc(S["drow_ready"], 1)
            pool.wait_ge(S["in_cond"], 16)
            link(g.tensor_copy(condf[:, :], condi[:, :]))
            g.tensor_scalar(onehot[:, :], condf[:, :], pcol[0:NK, 0:1], None, ALU.is_equal).then_inc(S["sel_oh"], 1)

            def band(k):
                link(g.tensor_scalar(ctmp[:, :], diff[:, :], float(GB * (TAPS // 2 - k)), cwt[:, k:k + 1], ALU.is_equal, ALU.mult))
                if k == 0:
                    link(g.tensor_copy(cmat[:, :], ctmp[:, :]))
                else:
                    link(g.tensor_tensor(cmat[:, :], cmat[:, :], ctmp[:, :], ALU.add))

            pool.wait_ge(S["in_cw"], 16)
            for k in range(EARLY_TAPS):
                band(k)
            g.memset(magV[:, :, 0:1], 1.0)
            link(g.memset(magU[:, :, 0:1], 1.0))
            pool.wait_ge(S["par_ready"], 1)
            g.tensor_tensor(tV[:, :, :], par[:, 3, :].unsqueeze(2).to_broadcast([P, H, RS]),
                            ramp[:, 0:RS].unsqueeze(1).to_broadcast([P, H, RS]), ALU.mult).then_inc(S["tV_ready"], 1)
            pows = [par[:, 2, :]]
            for k in range(8):
                link(g.tensor_tensor(sq[:, k, :], pows[k], pows[k], ALU.mult))
                pows.append(sq[:, k, :])
            for k in range(4):
                w = 1 << k
                link(g.tensor_tensor(magU[:, :, w:2 * w], magU[:, :, 0:w],
                                     pows[5 + k].unsqueeze(2).to_broadcast([P, H, w]), ALU.mult))
            for k in range(5):
                w = 1 << k
                last = g.tensor_tensor(magV[:, :, w:2 * w], magV[:, :, 0:w],
                                       pows[k].unsqueeze(2).to_broadcast([P, H, w]), ALU.mult)
                if k < 4:
                    link(last)
            last.then_inc(S["mags"], 1)
            pool.wait_ge(S["mags"], 1)
            for k in range(2):
                pool.wait_ge(S["sin_done"], k + 3)
                hs = slice(k * H // 2, (k + 1) * H // 2)
                g.tensor_tensor(sV[:, hs, :], sV[:, hs, :], magV[:, hs, :], ALU.mult).then_inc(S["kfac_v"], 1)
            pool.wait_ge(S["in_w"], 16)
            pool.wait_ge(S["delta_sb"], 4)
            for t in range(4):
                g.tensor_tensor(w_in[:, t, :], w_in[:, t, :], dlt[:, t, :], ALU.add).then_inc(S["raw_ready"], 1)
            for k in range(EARLY_TAPS, TAPS):
                band(k)
            pool.wait_ge(S["own_ready"], 1)
            pool.wait_ge(S["sel_loaded"], 16 * GB)
            link(g.tensor_tensor(gmat[:, :, :].rearrange("p g (d b) -> p (g d) b", b=GB),
                                 wrows[:, :, :].rearrange("p g d -> p (g d)").unsqueeze(2).to_broadcast([P, NG * H, GB]),
                                 own[:, :].unsqueeze(1).to_broadcast([P, NG * H, GB]), ALU.mult))
            g.tensor_tensor(gmat[:, :, :], gmat[:, :, :], ident[:, :].unsqueeze(1).to_broadcast([P, NG, P]), ALU.add
                            ).then_inc(S["gmat_ready"], 1)
            half = NC // 2 * NG * 2 * GB
            for i in range(NPAIR):
                pool.wait_ge(S["conv_used"], i + 1)
                if i > 0:
                    pool.wait_ge(S["mhalf_ready"], i)
                pair = xT[:, :, :, 2 * i:2 * i + 2, :].rearrange("p c g h b -> p (c g) h b")
                g.tensor_tensor(
                    mtmp.rearrange("p (n h b) -> p n h b", h=2, b=GB), pair,
                    mask2[:, :, :].rearrange("p c (g b) -> p (c g) b", b=GB).unsqueeze(2).to_broadcast([P, NC * NG, 2, GB]),
                    ALU.mult).then_inc(S["masked"], 1)
                pool.wait_ge(S["masked"], i + 1)
                if i >= 4:
                    pool.wait_ge(S["mhalf_used"], i - 3)
                g.tensor_tensor(mhalf[:, i % 4, :], mtmp[:, 0:half], mtmp[:, half:], ALU.add).then_inc(S["mhalf_ready"], 1)
                if i - 1 in POOL_LOWER:
                    pool.wait_ge(S["hi_ready"], i)
                    pair = slice(2 * i - 2, 2 * i)
                    g.tensor_tensor(x_lo[:, :, :, pair, :].rearrange("p c g h b -> p (c g) h b"),
                                    xT[:, :, :, pair, :].rearrange("p c g h b -> p (c g) h b"),
                                    x_hi[:, :, :, pair, :].bitcast(F32).rearrange("p c g h b -> p (c g) h b"),
                                    ALU.subtract).then_inc(S["lo_ready"], 1)

        @block.scalar
        def _(act):
            a = nc.scalar
            act.dma_start(lns[:, 0:1], bass.AP(log_dt.tensor, 0, [[0, GB], [1, H], [1, 1]])).then_inc(S["in_lns"], 16)
            act.dma_start(cb[:, :], bass.AP(codebook.tensor, 0, [[0, P], [1, NCODE]])).then_inc(S["in_cb"], 16)
            act.dma_start(lb[:, :, :], lora_B.rearrange("(t p) r -> p t r", p=P)).then_inc(S["in_lb"], 16)
            act.dma_start(la[:, :], lora_A).then_inc(S["in_la"], 16)
            act.dma_start(cwt[:, :], bass.AP(conv_w.tensor, 0, [[0, P], [1, TAPS]])).then_inc(S["in_cw"], 16)

            def x_evac(g):
                act.wait_ge(S["xt_done"], g + 1)
                dst = xT[:, :, g, :, :].rearrange("p c h b -> p c (h b)")
                a.copy(dst, x_banks[g % 4][:, :].rearrange("p (c n) -> p c n", c=NC)).then_inc(xt_sb[g % 4], 1)

            act.wait_ge(S["lbT_done"], 1)
            a.mul(lbT[:, :], psB[0:R, :], 0.5).then_inc(S["lbT_sb"], 1)
            act.wait_ge(S["tanh_in"], 1)
            a.activation(pm[:, 7, :], pm[:, 0, :], ACT.Tanh, scale=0.5).then_inc(S["tanh_done"], 1)
            act.wait_ge(S["trig_in"], 1)
            a.activation(pm[:, 6, :], pm[:, 4, :], ACT.Sin, scale=0.5).then_inc(S["trig_done"], 1)
            a.activation(pm[:, 5, :], pm[:, 4, :], ACT.Sin).then_inc(S["trig_done"], 1)
            def kernels_out(k, bank):
                act.wait_ge(S["k_done"], k + 1)
                hs = slice(k * H // 2, (k + 1) * H // 2)
                a.copy(ksb[:, hs, ::-1], bank[0:AS, :].rearrange("a (h r) -> a h r", r=RS)).then_inc(S["ksb_ready"], 1)
                act.wait_ge(S["ksb_ready"], k + 1)
                act.dma_start(bass.AP(kpad, k * (H // 2) * PAD, [[RS, AS], [PAD, H // 2], [1, RS]]),
                              ksb[:, hs, :]).then_inc(k_written[k], 16)

            def delta_evac(t):
                act.wait_ge(S["delta_done"], t + 1)
                a.copy(dlt[:, t, :], psC[t][:, :]).then_inc(S["delta_sb"], 1)

            delta_evac(0)
            delta_evac(1)
            delta_evac(2)
            delta_evac(3)
            for i in range(2):
                act.wait_ge(S["sel_done"], i + 1)
                a.copy(wsel[:, i * 512:(i + 1) * 512], psX[i][0:B, :]).then_inc(S["sel_sb"], 1)
            act.wait_ge(S["consts"], 1)
            for g in range(NG):
                if g == SIN_AT:
                    act.wait_ge(S["sinU_in"], 1)
                    a.activation(sU[:, 0, :, :], fU[:, 0, :, :], ACT.Sin, bias=quarter_rad[:, 0:1],
                                 scale=-TWO_PI).then_inc(S["sin_done"], 1)
                    act.wait_ge(S["sinU_in"], 2)
                    a.activation(sU[:, 1, :, :], fU[:, 1, :, :], ACT.Sin, scale=-TWO_PI).then_inc(S["sin_done"], 1)
                    act.wait_ge(S["sinV_in"], 1)
                    for k in range(2):
                        hs = slice(k * H // 2, (k + 1) * H // 2)
                        a.activation(sV[:, hs, :], fV[:, hs, :], ACT.Sin, bias=phase_rad[:, 0:1],
                                     scale=-TWO_PI).then_inc(S["sin_done"], 1)
                if g == X_BEFORE_K:
                    kernels_out(0, psA)
                    kernels_out(1, psB)
                if g not in X_ON_DVE:
                    x_evac(g)

            def upper(i):
                act.wait_ge(S["conv_used"], i + 1)
                a.copy(x_hi[:, :, :, 2 * i:2 * i + 2, :].rearrange("p c g h b -> p (c g) h b"),
                       xT[:, :, :, 2 * i:2 * i + 2, :].rearrange("p c g h b -> p (c g) h b")).then_inc(S["hi_ready"], 1)

            def scale_codes(t):
                act.wait_ge(S["ste_ready"], t + 1)
                for q in range(4):
                    last = a.activation(quant[:, t, q * P:(q + 1) * P], quant[:, t, q * P:(q + 1) * P], ACT.Copy,
                                        scale=ex[:, 4, 1 + N:][:, 4 * t + q:4 * t + q + 1])
                last.then_inc(S["scaled"], 1)

            def mt_upper(c):
                act.wait_ge(S["wT_done"], c + 1)
                a.copy(mt_hi[:, c, :], wT_banks[c][:, :]).then_inc(S["mt_hi_sb"], 1)

            for i in range(NPAIR):
                act.wait_ge(in_hank[i % NSLOT], 16 * (i // NSLOT + 1))
                if i >= NSLOT:
                    act.wait_ge(S["conv_done"], i - NSLOT + 1)
                if i == 0:
                    a.copy(toep[:, 0, 0, :], hank[:, 0, 0, ::-1]).then_inc(S["turned_first"], 1)
                    a.copy(toep[:, 0, 1, :], hank[:, 0, 1, ::-1]).then_inc(S["turned"], 1)
                else:
                    a.copy(toep[:, i % NSLOT, :, :], hank[:, i % NSLOT, :, ::-1]).then_inc(S["turned"], 1)
                if i >= UPPER_LAG:
                    upper(i - UPPER_LAG)
                if i in (9, 11, 13, 15):
                    scale_codes((i - 9) // 2)
            for i in range(NPAIR - UPPER_LAG, NPAIR - 1):
                upper(i)
            mt_upper(0)
            upper(NPAIR - 1)
            mt_upper(1)
            mt_upper(2)
            mt_upper(3)
            act.wait_ge(S["gmat_ready"], 1)
            act.wait_ge(S["weff"], 4)
            a.copy(g_hi[:, :, :], gmat[:, :, :]).then_inc(S["g_hi_ready"], 1)
            for g in range(NG):
                if g == 0:
                    act.wait_ge(S["chan"], 1)
                    a.activation(gth[:, :], psB[:, 0:NG], ACT.Tanh, scale=0.5).then_inc(S["gate_th"], 1)
                    act.wait_ge(S["gated"], 1)
                for step, part in enumerate(HALVES if g == NG - 1 else (ALL,)):
                    act.wait_ge(S["y_done"], g + step + 1)
                    if g >= 4:
                        act.wait_ge(S["o_done"], g - 3)
                    a.activation(y_hi[:, g % 4, part], psC[(g + step) % NB][:, part], ACT.Copy, scale=gate[:, g:g + 1]
                                 ).then_inc(S["y_hi_sb"], 1)
            for g, part in ((NG - 2, ALL), (NG - 1, HALVES[0])):
                act.wait_ge(S["o_done"], g + 1)
                act.wait_ge(stored[g % 8], 16 * (g // 8))
                a.copy(out_slots[g % 8][:, part], o_banks[g % 4][:, part]).then_inc(S["o_sb_act"], 1)

        @block.vector
        def _(dve):
            v = nc.vector
            n = {"par_chain": 0, "thr_chain": 0}

            def chained(name):
                def step(op, *args):
                    if n[name]:
                        dve.wait_ge(S[name], n[name])
                    op(*args).then_inc(S[name], 1)
                    n[name] += 1
                return step

            par_step, thr_step = chained("par_chain"), chained("thr_chain")

            mx, mn, cnt, rank, actc, tcol, ccol = (small[:, i:i + 1] for i in range(7))
            v.memset(tp[:, 0:1], -BIG)
            v.memset(tp[:, 64:65], BIG)

            y, k, r, p = (ex[:, i, :] for i in range(4))
            dve.wait_ge(S["in_lns"], 48)
            par_step(v.tensor_scalar, y, lns[:, :], -87.0, 88.0, ALU.max, ALU.min)
            dve.wait_ge(S["in_cb"], 16)
            thr_step(v.tensor_reduce, mx, cb[:, :], AX_X, ALU.max)
            par_step(v.tensor_scalar, k, y, 1.4426950408889634, ROUND, ALU.mult, ALU.add)
            thr_step(v.tensor_reduce, mn, cb[:, :], AX_X, ALU.min)
            par_step(v.tensor_scalar, k, k, ROUND, None, ALU.subtract)
            thr_step(v.scalar_tensor_tensor, mx, mn, -1.0, mx, ALU.mult, ALU.max)
            par_step(v.scalar_tensor_tensor, r, k, -LN2_HI, y, ALU.mult, ALU.add)
            thr_step(v.tensor_scalar, mx, mx, 1e-8, None, ALU.max)
            par_step(v.scalar_tensor_tensor, r, k, -LN2_LO, r, ALU.mult, ALU.add)
            thr_step(v.reciprocal, mx, mx)
            par_step(v.tensor_scalar, p, r, 1.0 / 5040, None, ALU.mult)
            thr_step(v.tensor_scalar, cb[:, :], cb[:, :], mx, None, ALU.mult)
            par_step(v.tensor_scalar, exi[:, :], k, 127.0, None, ALU.add)
            thr_step(v.tensor_tensor, th[:, 1:64], cb[:, 0:NTH], cb[:, 1:NCODE], ALU.add)
            par_step(v.tensor_scalar, exi[:, :], exi[:, :], 23, None, ALU.logical_shift_left)
            thr_step(v.tensor_scalar, th[:, 1:64], th[:, 1:64], 0.5, None, ALU.mult)

            def tree(level):
                s = 32 >> level
                return tp[:, s:64:2 * s], th[:, s:64:2 * s], tp[:, 0:64:2 * s], tp[:, 2 * s:65:2 * s]

            def clip_low(level):
                mid, own_th, low, _ = tree(level)
                thr_step(v.tensor_tensor, mid, own_th, low, ALU.max)

            def clip_high(level):
                mid, _, _, high = tree(level)
                thr_step(v.tensor_tensor, mid, mid, high, ALU.min)

            for level, c in ((0, 720), (1, 24), (2, 2)):
                par_step(v.scalar_tensor_tensor, p, p, 1.0 / c, r, ALU.add, ALU.mult)
                clip_low(level)
                par_step(v.scalar_tensor_tensor, p, p, 1.0 / {720: 120, 24: 6, 2: 1}[c], r, ALU.add, ALU.mult)
                clip_high(level)
            e = ex[:, 4, :]
            par_step(v.scalar_tensor_tensor, e, p, 1.0, exi[:, :].bitcast(F32), ALU.add, ALU.mult)
            clip_low(3)
            dt, aa = e[0:H, 0:1], e[0:H, 1:1 + N]
            scale = e[:, 1 + N:]

            xx, w, kk, wr, wc, s1, s2, tt = (pm[:, i, :] for i in (0, 1, 2, 3, 4, 5, 6, 7))
            bb = bim[0:H, :]
            dve.wait_ge(S["par_chain"], n["par_chain"])
            v.tensor_scalar(xx, aa, dt, -1.0, ALU.mult, ALU.mult).then_inc(S["tanh_in"], 1)
            dve.wait_ge(S["in_imag"], 16)
            par_step(v.tensor_scalar, w, bb, dt, None, ALU.mult)
            clip_high(3)
            par_step(v.tensor_scalar, kk, w, 0.15915494309189535, ROUND, ALU.mult, ALU.add)
            clip_low(4)
            par_step(v.tensor_scalar, kk, kk, ROUND, None, ALU.subtract)
            clip_high(4)
            par_step(v.scalar_tensor_tensor, wr, kk, -PI2_A, w, ALU.mult, ALU.add)
            clip_low(5)
            par_step(v.scalar_tensor_tensor, wr, kk, -PI2_B, wr, ALU.mult, ALU.add)
            clip_high(5)
            par_step(v.scalar_tensor_tensor, wr, kk, -PI2_C, wr, ALU.mult, ALU.add)
            thr_step(v.tensor_tensor, act_row[:, 0:NTH], tp[:, 1:64], tp[:, 2:65], ALU.is_lt)
            dve.wait_ge(S["par_chain"], n["par_chain"])
            v.tensor_scalar(wc, wr, -3.1415925, 3.1415925, ALU.max, ALU.min).then_inc(S["trig_in"], 1)
            em, q = pm[:, 11, :], pm[:, 13, :]
            dve.wait_ge(S["tanh_done"], 1)
            par_step(v.tensor_scalar, em, tt, -1.0, 1.0, ALU.mult, ALU.add)
            thr_step(v.tensor_reduce, cnt, act_row[:, 0:NTH], AX_X, ALU.add)
            par_step(v.reciprocal, em, em)
            v.tensor_scalar(pp[:, 3, 0:N], wr, 0.15915494309189535, None, ALU.mult)
            par_step(v.scalar_tensor_tensor, em, tt, 2.0, em, ALU.mult, ALU.mult)
            v.tensor_scalar(pp[:, 3, N:], wr, 0.15915494309189535, None, ALU.mult)
            ep = pp[:, 2, 0:N]
            par_step(v.tensor_scalar, pp[:, 2, 0:N], em, 1.0, None, ALU.add)
            v.tensor_scalar(pp[:, 2, N:], em, 1.0, None, ALU.add).then_inc(S["params"], 1)

            dve.wait_ge(S["consts"], 1)
            dve.wait_ge(S["thr_chain"], n["thr_chain"])
            v.tensor_tensor(scr[0:NTH, 0, 0:NTH], act_row[0:NTH, 0:NTH], tri[0:NTH, 0:NTH], ALU.mult)
            v.tensor_tensor(scr[0:NTH, 1, 0:NTH], act_row[0:NTH, 0:NTH], ident[0:NTH, 0:NTH], ALU.mult)
            v.tensor_tensor(scr[0:NTH, 2, 0:NTH], tp[0:NTH, 1:64], ident[0:NTH, 0:NTH], ALU.mult)
            thr_step(v.tensor_tensor, scr[0:NTH, 3, 0:NTH], cb[0:NTH, 1:NCODE], ident[0:NTH, 0:NTH], ALU.mult)

            dve.wait_ge(S["params_T"], 1)
            v.tensor_copy(par[:, 2:4, :], psA[:, 0:2 * H].rearrange("p (k h) -> p k h", h=H)).then_inc(S["par_ready"], 1)
            a2, b2, inv = (pm[:, i, :] for i in (8, 9, 10))
            v.tensor_tensor(a2, aa, aa, ALU.mult)
            par_step(v.tensor_tensor, b2, bb, bb, ALU.mult)
            dve.wait_ge(S["trig_done"], 1)
            par_step(v.tensor_tensor, q, s2, s2, ALU.mult)
            v.tensor_tensor(a2, a2, b2, ALU.add)
            par_step(v.scalar_tensor_tensor, q, q, 2.0, ep, ALU.mult, ALU.mult)
            v.tensor_reduce(small[0:NTH, 3:7], scr[0:NTH, :, 0:NTH], AX_X, ALU.add).then_inc(S["thr_chain"], 1)
            n["thr_chain"] += 1
            dve.wait_ge(S["par_chain"], n["par_chain"])
            v.tensor_tensor(pm[:, 14, :], em, q, ALU.subtract)
            dve.wait_ge(S["trig_done"], 2)
            par_step(v.tensor_tensor, pm[:, 15, :], ep, s1, ALU.mult)
            thr_step(v.tensor_scalar, small[0:NTH, 5:7], small[0:NTH, 5:7], actc[0:NTH, :], None, ALU.mult)
            par_step(v.reciprocal, inv, a2)
            E = pm[:, 14:16, :]
            aE, bE, G, c0G, c1G = pm[:, 16:18, :], pm[:, 18:20, :], pm[:, 20:22, :], pm[:, 22:24, :], pm[:, 0:2, :]
            a_b = aa.unsqueeze(1).to_broadcast([H, 2, N])
            b_b = bb.unsqueeze(1).to_broadcast([H, 2, N])
            v.tensor_tensor(aE, E, a_b, ALU.mult)
            par_step(v.tensor_tensor, bE, E, b_b, ALU.mult)
            thr_step(v.tensor_scalar, slot_rhs[0:NTH, 0, :], ramp1[0:NTH, :], rank[0:NTH, :], tcol[0:NTH, :], ALU.is_equal, ALU.mult)
            dve.wait_ge(S["par_chain"], n["par_chain"])
            v.tensor_tensor(pm[:, 20, :], pm[:, 19, :], pm[:, 16, :], ALU.subtract)
            par_step(v.tensor_tensor, pm[:, 21, :], pm[:, 18, :], pm[:, 17, :], ALU.add)
            thr_step(v.tensor_scalar, slot_rhs[0:NTH, 1, :], ramp1[0:NTH, :], rank[0:NTH, :], ccol[0:NTH, :], ALU.is_equal, ALU.mult)
            par_step(v.scalar_tensor_tensor, G, G, 2.0, inv.unsqueeze(1).to_broadcast([H, 2, N]), ALU.mult, ALU.mult)
            v.tensor_copy(n_int[:, :], cnt)
            dve.wait_ge(S["in_c"], 16)
            c0 = cin[0:H, :, 0].unsqueeze(1).to_broadcast([H, 2, N])
            c1 = cin[0:H, :, 1].unsqueeze(1).to_broadcast([H, 2, N])
            dve.wait_ge(S["par_chain"], n["par_chain"])
            v.tensor_tensor(c0G, G, c0, ALU.mult)
            par_step(v.tensor_tensor, c1G, G, c1, ALU.mult)
            dve.wait_ge(S["thr_chain"], n["thr_chain"])
            v.tensor_scalar(over[:, :], ramp1[:, :], cnt, BIG, ALU.is_gt, ALU.mult).then_inc(S["slot_ready"], 1)
            dve.wait_ge(S["par_chain"], n["par_chain"])
            v.tensor_tensor(pp[:, 0, N:], pm[:, 23, :], pm[:, 0, :], ALU.subtract)
            v.tensor_tensor(pp[:, 1, 0:N], pm[:, 23, :], pm[:, 0, :], ALU.subtract)
            par_step(v.tensor_tensor, pp[:, 0, 0:N], pm[:, 22, :], pm[:, 1, :], ALU.add)
            v.reciprocal(inv_scale[:, :], scale).then_inc(S["scale_ready"], 1)
            dve.wait_ge(S["par_chain"], n["par_chain"])
            v.tensor_scalar(pp[:, 1, N:], pp[:, 0, 0:N], -1.0, None, ALU.mult).then_inc(S["params"], 1)

            tau, tw = par[:, 3, :], tau32[:, 0, :]
            dve.wait_ge(S["par_ready"], 1)
            par_step(v.tensor_scalar, tau32[:, 1, :], tau, 32.0, ROUND, ALU.mult, ALU.add)
            par_step(v.tensor_scalar, tau32[:, 1, :], tau32[:, 1, :], ROUND, None, ALU.subtract)
            par_step(v.scalar_tensor_tensor, tw, tau, 32.0, tau32[:, 1, :], ALU.mult, ALU.subtract)
            par_step(v.tensor_tensor, tU[:, :, :], tw.unsqueeze(2).to_broadcast([P, H, AS]),
                     ramp[:, 0:AS].unsqueeze(1).to_broadcast([P, H, AS]), ALU.mult)
            par_step(v.tensor_scalar, fU[:, 0, :, :], tU[:, :, :], 0.25, ROUND, ALU.add, ALU.add)
            v.tensor_scalar(fU[:, 1, :, :], tU[:, :, :], ROUND, None, ALU.add).then_inc(S["par_chain"], 1)
            dve.wait_ge(S["par_chain"], n["par_chain"])
            v.scalar_tensor_tensor(fU[:, 0, :, :], fU[:, 0, :, :], ROUND, tU[:, :, :], ALU.subtract, ALU.subtract).then_inc(S["sinU_in"], 1)
            n["par_chain"] += 1
            dve.wait_ge(S["par_chain"], n["par_chain"])
            v.scalar_tensor_tensor(fU[:, 1, :, :], fU[:, 1, :, :], ROUND, tU[:, :, :], ALU.subtract, ALU.subtract).then_inc(S["sinU_in"], 1)
            dve.wait_ge(S["tV_ready"], 1)
            thr_step(v.tensor_scalar, fV[:, :, :], tV[:, :, :], phase[:, 0:1], ROUND, ALU.add, ALU.add)
            dve.wait_ge(S["thr_chain"], n["thr_chain"])
            v.scalar_tensor_tensor(fV[:, :, :], fV[:, :, :], ROUND, tV[:, :, :], ALU.subtract, ALU.subtract).then_inc(S["sinV_in"], 1)

            dve.wait_ge(S["params_T"], 2)
            par_step(v.tensor_copy, par[:, 0:2, :], psC[3][:, 0:2 * H].rearrange("p (k h) -> p k h", h=H))
            dve.wait_ge(S["sin_done"], 2)
            dve.wait_ge(S["mags"], 1)
            for k in range(2):
                hs = slice(k * H // 2, (k + 1) * H // 2)
                al = par[:, 0, hs].unsqueeze(2).to_broadcast([P, H // 2, AS])
                be = par[:, 1, hs].unsqueeze(2).to_broadcast([P, H // 2, AS])
                dve.wait_ge(S["par_chain"], n["par_chain"])
                v.tensor_tensor(sU[:, 0, hs, :], sU[:, 0, hs, :], al, ALU.mult)
                par_step(v.tensor_tensor, sU[:, 1, hs, :], sU[:, 1, hs, :], be, ALU.mult)
                par_step(v.tensor_tensor, sU[:, 0, hs, :], sU[:, 0, hs, :], sU[:, 1, hs, :], ALU.add)
                dve.wait_ge(S["par_chain"], n["par_chain"])
                v.tensor_tensor(tU[:, hs, ::-1], sU[:, 0, hs, :], magU[:, hs, :], ALU.mult).then_inc(S["kfac"], 1)

            m = [0]

            def link(ins):
                m[0] += 1
                ins.then_inc(S["dve_chain"], 1)
                dve.wait_ge(S["dve_chain"], m[0])

            v.tensor_reduce(own[:, :], ident[:, :].rearrange("p (h b) -> p b h", b=GB), AX_X, ALU.add).then_inc(S["own_ready"], 1)
            dve.wait_ge(S["in_len"], 32)
            par_step(v.tensor_copy, lenf[:, :, :], leni[:, :, :])
            dve.wait_ge(S["par_chain"], n["par_chain"])
            for c in range(NC):
                v.tensor_scalar(keep[:, c, :], lenf[:, 0, :], pcol[:, 0:1], float(P * c), ALU.subtract, ALU.is_gt)
                last = v.tensor_scalar(mask2[:, c, :], lenf[:, 1, :], pcol[:, 0:1], float(P * c), ALU.subtract, ALU.is_gt)
            last.then_inc(S["masks"], 1)

            def x_evac(g):
                dve.wait_ge(S["xt_done"], g + 1)
                v.tensor_copy(xT[:, :, g, :, :].rearrange("p c h b -> p c (h b)"),
                              x_banks[g % 4][:, :].rearrange("p (c n) -> p c n", c=NC)).then_inc(xt_sb[g % 4], 1)

            v.tensor_copy(quant[:, :, :], cb[:, 0:1].unsqueeze(2).to_broadcast([P, 4, L]))
            dve.wait_ge(S["own_ready"], 1)
            par_step(v.reciprocal, linv[:, :], lenf[:, 1, :])
            par_step(v.tensor_tensor, lown[:, :, :], linv[:, :].rearrange("p (g b) -> p g b", b=GB),
                     own[:, :].unsqueeze(1).to_broadcast([P, NG, GB]), ALU.mult)
            par_step(v.tensor_reduce, linv_own[:, :], lown[:, :, :], AX_X, ALU.add)
            x_evac(X_ON_DVE[0])
            x_evac(X_ON_DVE[1])
            dve.wait_ge(S["slot_done"], 1)
            v.tensor_copy(slots[:, :, :], psC[2][:, 0:128].rearrange("p (k j) -> p k j", k=2)).then_inc(S["slots_sb"], 1)
            dve.wait_ge(S["slots_sb"], 1)
            link(v.tensor_tensor(slots[:, 0, :], slots[:, 0, :], over[:, :], ALU.add))
            dve.wait_ge(S["scale_ready"], 1)
            for t in range(4):
                if t < len(X_ON_DVE) - 2:
                    x_evac(X_ON_DVE[2 + t])
                dve.wait_ge(S["raw_ready"], t + 1)
                link(v.tensor_tensor(nrm[:, t, :].rearrange("p (g k) -> p g k", k=P), w_in[:, t, :].rearrange("p (g k) -> p g k", k=P),
                                     inv_scale[:, 4 * t:4 * t + 4].unsqueeze(2).to_broadcast([P, 4, P]), ALU.mult))
            def merge(i):
                dve.wait_ge(S["conv_done"], i + 1)
                dst = xT[:, :, :, 2 * i:2 * i + 2, :].rearrange("p c g h b -> p h (c g) b")
                kp = keep[:, :, :].rearrange("p c (g b) -> p (c g) b", b=GB).unsqueeze(1).to_broadcast([P, 2, NC * NG, GB])
                v.copy_predicated(dst, kp, psC[i % 4][:, :].rearrange("p (h n b) -> p h n b", h=2, b=GB)
                                  ).then_inc(S["conv_used"], 1)

            merged = 0
            for j in range(FAST_SLOTS):
                link(v.tensor_scalar(msk[:, :, :], nrm[:, :, :], slots[:, 0, j:j + 1], None, ALU.is_gt))
                link(v.copy_predicated(quant[:, :, :], msk[:, :, :],
                                       slots[:, 1, j:j + 1].unsqueeze(2).to_broadcast([P, 4, L])))
                if j == 0:
                    dve.wait_ge(S["masks"], 1)
                    for b in range(4):
                        dve.wait_ge(xt_sb[b], NG // 4)
                for _ in range(MERGES[j] if j < len(MERGES) else 0):
                    merge(merged)
                    merged += 1
            n_slots = dve.value_load(n_int[0:1, 0:1], min_val=1, max_val=NTH)
            with dve.If(n_slots > FAST_SLOTS):
                with dve.Fori(FAST_SLOTS, NTH) as j:
                    v.tensor_copy(cur[:, 0:2], slots[:, :, bass.ds(j, 1)].rearrange("p a b -> p (a b)")).then_inc(S["dve_loop"], 1)
                    dve.wait_ge(S["dve_loop"], j * 3 - (3 * FAST_SLOTS - 1))
                    v.tensor_scalar(msk[:, :, :], nrm[:, :, :], cur[:, 0:1], None, ALU.is_gt).then_inc(S["dve_loop"], 1)
                    dve.wait_ge(S["dve_loop"], j * 3 - (3 * FAST_SLOTS - 2))
                    v.tensor_copy(cur[:, 2:3], cur[:, 0:1])
                    v.copy_predicated(quant[:, :, :], msk[:, :, :],
                                      cur[:, 1:2].unsqueeze(2).to_broadcast([P, 4, L])).then_inc(S["dve_loop"], 1)
                    dve.wait_ge(S["dve_loop"], j * 3 - (3 * FAST_SLOTS - 3))

            def straight_through(t):
                q, m = quant[:, t, :], nrm[:, t, :]
                link(v.tensor_tensor(q, q, m, ALU.subtract))
                v.tensor_tensor(q, q, m, ALU.add).then_inc(S["ste_ready"], 1)

            def weff(t):
                q = quant[:, t, :]
                dve.wait_ge(S["scaled"], t + 1)
                link(v.tensor_tensor(q, q, dlt[:, t, :], ALU.add))
                qd = q[:, t * P:(t + 1) * P]
                v.tensor_tensor(qd, qd, ident[:, :], ALU.add).then_inc(S["weff"], 1)

            def add_halves(i):
                dve.wait_ge(S["mhalf_ready"], i + 1)
                h2 = mhalf[:, i % 4, :].rearrange("p (k g n) -> p k g n", k=2, g=NG)
                dst = msum[:, :, 2 * i * GB:(2 * i + 2) * GB]
                v.tensor_tensor(dst, h2[:, 0], h2[:, 1], ALU.add).then_inc(S["mhalf_used"], 1)

            def lower(i):
                dve.wait_ge(S["hi_ready"], i + 1)
                dve.wait_ge(S["masked"], i + 1)
                pair = slice(2 * i, 2 * i + 2)
                v.tensor_tensor(x_lo[:, :, :, pair, :].rearrange("p c g h b -> p (c g) h b"),
                                xT[:, :, :, pair, :].rearrange("p c g h b -> p (c g) h b"),
                                x_hi[:, :, :, pair, :].bitcast(F32).rearrange("p c g h b -> p (c g) h b"),
                                ALU.subtract).then_inc(S["lo_ready"], 1)

            def mt_lower(c):
                dve.wait_ge(S["mt_hi_sb"], c + 1)
                v.tensor_tensor(mt_lo[:, c, :], wT_banks[c][:, :], mt_hi[:, c, :].bitcast(F32), ALU.subtract).then_inc(S["mt_lo_sb"], 1)

            for i in range(merged - 3):
                add_halves(i)
            for i in range(merged, NPAIR):
                if i in (8, 10, 12, 14):
                    weff((i - 8) // 2)
                merge(i)
                if i >= 3:
                    add_halves(i - 3)
                if i == merged + 2:
                    for k in range(merged + 2 - UPPER_LAG):
                        if k not in POOL_LOWER:
                            lower(k)
                k = i - UPPER_LAG
                if i >= merged + 2 and k not in POOL_LOWER and k < LATE_LOWER:
                    lower(k)
                if i in (5, 7, 9, 11):
                    straight_through((i - 5) // 2)
            def matrices_lower(k):
                dve.wait_ge(S["g_hi_ready"], 1)
                q = slice(4 * k, 4 * k + 4)
                v.tensor_tensor(g_lo[:, q, :], gmat[:, q, :], g_hi[:, q, :].bitcast(F32), ALU.subtract).then_inc(S["g_lo_ready"], 1)

            middle = (LATE_LOWER + NPAIR) // 2
            for i in range(LATE_LOWER, middle):
                lower(i)
            for c in range(NC):
                mt_lower(c)
            for i in range(NPAIR - 3, NPAIR):
                add_halves(i)
            for i in range(middle, NPAIR):
                lower(i)
            dve.wait_ge(S["par_chain"], n["par_chain"])
            for k in range(4):
                dve.wait_ge(S["ymean"], k + 1)
                v.tensor_reduce(gsum[:, 4 * k:4 * k + 4], mean_banks[k][:, :].rearrange("p (g n) -> p g n", n=P), AX_X, ALU.add
                                ).then_inc(S["gsum_ready"], 1)
            dve.wait_ge(S["gsum_ready"], 4)
            v.tensor_tensor(gmean[:, :], gsum[:, :], linv_own[:, :], ALU.mult).then_inc(S["gmean_ready"], 1)
            matrices_lower(0)
            dve.wait_ge(S["gate_th"], 1)
            v.tensor_scalar(gate[:, :], gth[:, :], 0.5, 1.5, ALU.mult, ALU.add).then_inc(S["gated"], 1)
            dve.wait_ge(S["gated"], 1)

            def y_lower(g, part=ALL, step=0):
                dve.wait_ge(S["y_hi_sb"], g + step + 1)
                v.scalar_tensor_tensor(y_lo[:, g % 4, part], psC[(g + step) % NB][:, part], gate[:, g:g + 1], y_hi[:, g % 4, part].bitcast(F32),
                                       ALU.mult, ALU.subtract).then_inc(S["y_sb"], 1)

            def out_rows(g, part=ALL, step=0):
                dve.wait_ge(S["o_done"], g + step + 1)
                if g >= 8:
                    dve.wait_ge(stored[g % 8], 16 * (g // 8))
                v.tensor_copy(out_slots[g % 8][:, part], o_banks[(g + step) % 4][:, part]).then_inc(S["o_sb"], 1)

            for g in range(NG):
                for k in range(mixed_before(g - 1), mixed_before(g)):
                    out_rows(k)
                if g == NG - 1:
                    y_lower(g, HALVES[0])
                    y_lower(g, HALVES[1], 1)
                else:
                    y_lower(g)
                if 1 <= g < 4:
                    matrices_lower(g)
            out_rows(NG - 1, HALVES[1], 1)

        @block.tensor
        def _(pe):
            m = nc.tensor
            pe.wait_ge(S["consts"], 1)
            pe.wait_ge(S["in_lb"], 16)
            for t in range(4):
                last = m.transpose(psB[0:R, t * P:(t + 1) * P], lb[:, t, :], ident[:, :])
            last.then_inc(S["lbT_done"], 1)
            pe.wait_ge(S["in_la"], 16)
            pe.wait_ge(S["lbT_sb"], 1)
            def delta(t):
                m.matmul(psC[t][:, :], lbT[:, t * P:(t + 1) * P], la[:, :], start=True, stop=True).then_inc(S["delta_done"], 1)

            def x_transposes(g):
                pe.wait_ge(in_x[g], 16)
                if g >= 4:
                    pe.wait_ge(xt_sb[g % 4], g // 4)
                elif g < 2:
                    pe.wait_ge(S["sel_sb"], g + 1)
                else:
                    pe.wait_ge(S["delta_sb"], g - 1)
                for c in range(NC):
                    last = m.transpose(x_banks[g % 4][:, c * P:(c + 1) * P], xrows[:, g, c * P:(c + 1) * P], ident[:, :])
                last.then_inc(S["xt_done"], 1)

            def param_transposes(k0, bank, n):
                pe.wait_ge(S["params"], n)
                for k in range(k0, k0 + 2):
                    last = m.transpose(bank[:, (k - k0) * H:(k - k0 + 1) * H], pp[:, k, :], ident[0:H, 0:H])
                last.then_inc(S["params_T"], 1)

            def d_at_zero():
                pe.wait_ge(S["drow_ready"], 1)
                pe.wait_ge(S["par_ready"], 1)
                for k, bank in ((0, psA), (1, psB)):
                    m.matmul(bank[0:AS, :], last_a[0:1, :], drow[:, k * H // 2:(k + 1) * H // 2, :].rearrange("p h r -> p (h r)"),
                             start=True, stop=False, skip_group_check=True)

            delta(0)
            delta(1)
            param_transposes(2, psA, 1)
            delta(2)
            delta(3)
            pe.wait_ge(S["sel_oh"], 1)
            pe.wait_ge(S["in_wall"], 16)
            for i in range(2):
                m.matmul(psX[i][0:B, :], onehot[:, :], wall[:, i * 512:(i + 1) * 512], start=True, stop=True).then_inc(S["sel_done"], 1)
            pe.wait_ge(S["delta_sb"], 4)
            param_transposes(0, psC[3], 2)
            d_at_zero()
            for g in range(X_BEFORE_K):
                x_transposes(g)
            for k, bank in ((0, psA), (1, psB)):
                pe.wait_ge(S["kfac_v"], k + 1)
                pe.wait_ge(S["kfac"], k + 1)
                for j in range(H // 2):
                    h = k * H // 2 + j
                    last = m.matmul(bank[0:AS, j * RS:(j + 1) * RS], tU[:, h, :], sV[:, h, :],
                                    start=False, stop=True, skip_group_check=True)
                last.then_inc(S["k_done"], 1)
            pe.wait_ge(S["slot_ready"], 1)
            m.matmul(psC[2][:, 0:128], ones[0:NTH, :], slot_rhs[0:NTH, :, :].rearrange("p k j -> p (k j)"),
                     start=True, stop=True).then_inc(S["slot_done"], 1)
            for g in range(X_BEFORE_K, NG):
                x_transposes(g)
            def weff_transposes(c):
                if c == 0:
                    pe.wait_ge(S["weff"], 4)
                for t in range(4):
                    last = m.transpose(wT_banks[c][:, t * P:(t + 1) * P], quant[:, t, c * P:(c + 1) * P], ident[:, :])
                last.then_inc(S["wT_done"], 1)

            for b in range(4):
                pe.wait_ge(xt_sb[b], NG // 4)
            for i in range(NPAIR):
                if i == 2:
                    pe.wait_ge(S["slots_sb"], 1)
                if i >= 4:
                    pe.wait_ge(S["conv_used"], i - 3)
                for j in range(2):
                    if i == 0 and j == 0:
                        pe.wait_ge(S["turned_first"], 1)
                    else:
                        pe.wait_ge(S["turned"], i + 1)
                    h = 2 * i + j
                    xh = xT[:, :, :, h, :].rearrange("p c g b -> p (c g) b")
                    for d in range(NC):
                        n = (NC - d) * B
                        o = j * NC * B + d * B
                        last = m.matmul(psC[i % 4][:, o:o + n], toep[:, i % NSLOT, j, d * P:(d + 1) * P], xh[:, 0:n // GB, :],
                                        start=(d == 0), stop=(d == NC - 1), skip_group_check=True)
                last.then_inc(S["conv_done"], 1)
            for c in range(NC):
                weff_transposes(c)

            def rows(part, g, c):
                return part[:, c, g, :, :].rearrange("p h b -> p (h b)")

            def upper_upper(g, c, part=ALL, step=0):
                m.matmul(psC[(g + step) % NB][:, part], rows(x_hi, g, c), mt_hi[:, c, part], start=(c == 0), stop=False)

            def upper_lower(g, c, part=ALL, step=0):
                m.matmul(psC[(g + step) % NB][:, part], rows(x_hi, g, c), mt_lo[:, c, part], start=False, stop=False)

            def lower_upper(g, part=ALL, step=0):
                for c in range(NC):
                    last = m.matmul(psC[(g + step) % NB][:, part], rows(x_lo, g, c), mt_hi[:, c, part], start=False, stop=(c == NC - 1))
                last.then_inc(S["y_done"], 1)

            def mix(g, part=ALL, step=0):
                pe.wait_ge(S["y_hi_sb"], g + step + 1)
                if g >= 4:
                    pe.wait_ge(S["o_sb"], g + step - 3)
                bank = o_banks[(g + step) % 4]
                m.matmul(bank[:, part], g_hi[:, g, :], y_hi[:, g % 4, part], start=True, stop=False)
                pe.wait_ge(S["g_lo_ready"], g // 4 + 1)
                m.matmul(bank[:, part], g_lo[:, g, :], y_hi[:, g % 4, part], start=False, stop=False)
                pe.wait_ge(S["y_sb"], g + step + 1)
                m.matmul(bank[:, part], g_hi[:, g, :], y_lo[:, g % 4, part], start=False, stop=True).then_inc(S["o_done"], 1)

            pe.wait_ge(S["hi_ready"], NPAIR)
            for c in range(NC):
                pe.wait_ge(S["mt_hi_sb"], c + 1)
                for g in range(NB):
                    upper_upper(g, c)
            for c in range(NC):
                if c == NC - 1:
                    pe.wait_ge(S["mt_lo_sb"], NC)
                    pe.wait_ge(S["mhalf_used"], NPAIR)
                    for k in range(4):
                        for g in range(4):
                            last = m.transpose(mean_banks[k][:, g * P:(g + 1) * P], msum[:, 4 * k + g, :], ident[:, :])
                        last.then_inc(S["ymean"], 1)
                pe.wait_ge(S["mt_lo_sb"], c + 1)
                for g in range(NB):
                    upper_lower(g, c)
            pe.wait_ge(S["lo_ready"], NPAIR)
            lower_upper(0)
            lower_upper(1)
            pe.wait_ge(S["g_hi_ready"], 1)
            pe.wait_ge(S["gmean_ready"], 1)
            m.matmul(psB[:, 0:NG], cmat[:, :], gmean[:, :], start=True, stop=True).then_inc(S["chan"], 1)
            lower_upper(2)
            lower_upper(3)
            for g in range(NB, NG):
                for k in range(mixed_before(g - 1), mixed_before(g)):
                    mix(k)
                pe.wait_ge(S["y_sb"], g - NB + 1)
                for step, part in enumerate(HALVES if g == NG - 1 else (ALL,)):
                    for c in range(NC):
                        upper_upper(g, c, part, step)
                        upper_lower(g, c, part, step)
                    lower_upper(g, part, step)
            for g in range(mixed_before(NG - 1), NG - 1):
                mix(g)
            for step in range(2):
                mix(NG - 1, HALVES[step], step)


_INS = ['x', 'itok_B_78_3631', 'itok_B_9_3973', 'condB_codebook', 'itok_B_0_15', 'L0_cond_log_dt', 'L0_cond_C',
        'L0_cond_log_A_real', 'L0_cond_A_imag', 'L0_cond_D', 'L1_cond_conv_w', 'L2_cond_weight', 'L2_cond_scale_log',
        'L2_cond_lora_A', 'L2_cond_lora_B', 'L3_cond_weights']
_OUTS = [((64, 32, 512), 'float32')]


def kernel(**inputs):
    import numpy as _np
    import concourse.bacc as _bacc
    from concourse import mybir as _mybir
    from concourse.bass_utils import run_bass_kernel_spmd as _run

    nc = _bacc.Bacc("TRN2", target_bir_lowering=False, num_devices=1)
    arrays, args = {}, []
    for name in _INS:
        a = _np.ascontiguousarray(inputs[name])
        arrays[f"in_{name}_dram"] = a
        args.append(nc.dram_tensor(f"in_{name}_dram", a.shape, _mybir.dt.from_np(a.dtype), kind="ExternalInput").ap())
    for i, (shape, dtype) in enumerate(_OUTS):
        dt = _mybir.dt.from_np(_np.dtype(dtype))
        args.append(nc.dram_tensor(f"out_{i}_dram", shape, dt, kind="ExternalOutput").ap())
    cond_resid_kernel(nc, *args)
    r = _run(nc, [arrays], core_ids=[0])
    got = tuple(r.results[0][f"out_{i}_dram"] for i in range(len(_OUTS)))
    return got[0]
```
